# Optimizing a Trainium2 kernel written in Bass

```python
import numpy as np
import jax
import jax.numpy as jnp

def _softmax(x, axis=-1):
    return jax.nn.softmax(x, axis=axis)

def _gelu(x):
    return jax.nn.gelu(x, approximate=True)

def _silu(x):
    return jax.nn.silu(x)

def _sigmoid(x):
    return jax.nn.sigmoid(x)

def _layernorm(x, axis=-1, eps=1e-05):
    m = jnp.mean(x, axis=axis, keepdims=True)
    v = jnp.var(x, axis=axis, keepdims=True)
    return (x - m) / jnp.sqrt(v + eps)

def _scatter_add(tgt, idx, src, axis=0):
    return tgt.at[idx].add(src)

def _segment_sum(src, seg, n):
    return jax.ops.segment_sum(src, seg, n)
kernel_name = 'mk_xattn_ffn_d2_seqx_r4_d4caa7'

def setup_inputs(seed: int=0):
    np.random.seed(seed)
    _w = jnp.asarray

    def _rec_inputs():
        import jax
        import jax.numpy as jnp
        _rk = jax.random.key(seed)
        x = 0.0002417 + 0.9998 * jax.random.normal(jax.random.fold_in(_rk, 1), (32, 112, 256), jnp.float32)
        _lenS = 112 - jax.random.randint(jax.random.fold_in(_rk, 7), (32,), 0, max(1, 112 // 4) + 1, jnp.int32)
        _lenS2 = 375 - jax.random.randint(jax.random.fold_in(_rk, 8), (32,), 0, max(1, 375 // 4) + 1, jnp.int32)
        _ctx_1024P = jax.random.normal(jax.random.fold_in(_rk, 11), (32, 16, 256), jnp.float32)
        _ctx_1024c = jax.random.dirichlet(jax.random.fold_in(_rk, 511), 0.3 * jnp.ones((16,), jnp.float32), (32, 375))
        _ctx_1024t = jnp.einsum('bsk,bkd->bsd', _ctx_1024c, _ctx_1024P)
        _ctx_1024t = _ctx_1024t * jax.lax.rsqrt(jnp.mean(jnp.square(_ctx_1024t)) + 1e-12) * 0.953939
        ctx_1024 = 7.22013e-05 + 1.00017 * (_ctx_1024t + 0.3 * jax.random.normal(jax.random.fold_in(_rk, 611), (32, 375, 256), jnp.float32))
        return (x, ctx_1024)
    x, ctx_1024 = _rec_inputs()

    def _L0_xattn_setup():
        import jax, jax.numpy as jnp
        import numpy as np
        D_MODEL = 256
        B, S = (4, 512)
        key = jax.random.key(seed)
        ks = jax.random.split(key, 10)
        s = 1.0 / np.sqrt(D_MODEL)
        return {'k': jax.random.normal(ks[0], (B, S, D_MODEL), jnp.float32), 'v': jax.random.normal(ks[1], (B, S, D_MODEL), jnp.float32), 'q': jax.random.normal(ks[2], (B, S, D_MODEL), jnp.float32), 'Wk': jax.random.normal(ks[3], (D_MODEL, D_MODEL), jnp.float32) * s, 'Wv': jax.random.normal(ks[4], (D_MODEL, D_MODEL), jnp.float32) * s, 'bv': jnp.zeros((D_MODEL,), jnp.float32), 'Wq': jax.random.normal(ks[5], (D_MODEL, D_MODEL), jnp.float32) * s, 'bq': jnp.zeros((D_MODEL,), jnp.float32), 'Wo': jax.random.normal(ks[6], (D_MODEL, D_MODEL), jnp.float32) * s, 'bo': jnp.zeros((D_MODEL,), jnp.float32)}
    _L0_xattn_all = _L0_xattn_setup()
    _L0_xattn_in = {k: v for k, v in _L0_xattn_all.items() if k in ('Wk', 'Wv', 'bv', 'Wq', 'bq', 'Wo', 'bo')}
    del _L0_xattn_all

    def _L0_ffn_setup():
        import jax, jax.numpy as jnp
        import numpy as np
        H = 256
        M = 128
        E = 16
        TOP_K = 4
        N_GROUP = 4
        TOPK_GROUP = 2
        SCALE = 2.5
        B, S = (2, 256)

        def _gate(x2d, gate_kernel, gate_bias):
            n = x2d.shape[0]
            logits = jnp.dot(x2d.astype(jnp.float32), gate_kernel.astype(jnp.float32))
            scores = jax.nn.sigmoid(logits)
            scores_for_choice = scores + gate_bias
            group_scores = scores_for_choice.reshape(n, N_GROUP, E // N_GROUP)
            top2 = jax.lax.top_k(group_scores, k=2)[0]
            group_sum = jnp.sum(top2, axis=-1)
            group_idx = jax.lax.top_k(group_sum, k=TOPK_GROUP)[1]
            group_mask = jnp.zeros_like(group_sum).at[jnp.arange(n)[:, None], group_idx].set(1.0)
            score_mask = jnp.repeat(group_mask[:, :, None], E // N_GROUP, axis=2).reshape(n, E)
            masked_scores = jnp.where(score_mask > 0, scores_for_choice, 0.0)
            topk_weight, topk_idx = jax.lax.top_k(masked_scores, k=TOP_K)
            topk_weight = topk_weight / (jnp.sum(topk_weight, axis=-1, keepdims=True) + 1e-20)
            topk_weight = topk_weight * SCALE
            return (topk_idx, topk_weight)
        key = jax.random.key(seed)
        ks = jax.random.split(key, 9)
        sc_h = 1.0 / np.sqrt(H)
        sc_m = 1.0 / np.sqrt(M)
        return {'hidden_states': jax.random.normal(ks[0], (B, S, H), jnp.float32), 'gate_kernel': jax.random.normal(ks[1], (H, E), jnp.float32) * sc_h, 'gate_bias': jax.random.normal(ks[2], (E,), jnp.float32) * 0.01, 'w_gate': jax.random.normal(ks[3], (E, H, M), jnp.float32) * sc_h, 'w_up': jax.random.normal(ks[4], (E, H, M), jnp.float32) * sc_h, 'w_down': jax.random.normal(ks[5], (E, M, H), jnp.float32) * sc_m, 'sw_gate': jax.random.normal(ks[6], (H, 2 * M), jnp.float32) * sc_h, 'sw_up': jax.random.normal(ks[7], (H, 2 * M), jnp.float32) * sc_h, 'sw_down': jax.random.normal(ks[8], (2 * M, H), jnp.float32) * (1.0 / np.sqrt(2 * M))}
    _L0_ffn_all = _L0_ffn_setup()
    _L0_ffn_in = {k: v for k, v in _L0_ffn_all.items() if k in ('gate_kernel', 'gate_bias', 'w_gate', 'w_up', 'w_down', 'sw_gate', 'sw_up', 'sw_down')}
    del _L0_ffn_all

    def _L1_xattn_setup():
        import jax, jax.numpy as jnp
        import numpy as np
        EMBED_DIM = 256
        NUM_HEADS = 16
        HEAD_DIM = EMBED_DIM // NUM_HEADS
        key = jax.random.key(seed)
        ks = jax.random.split(key, 11)
        s = 1.0 / np.sqrt(EMBED_DIM)
        inp = {'query': jax.random.normal(ks[0], (4, 512, EMBED_DIM), jnp.float32), 'key': jax.random.normal(ks[1], (4, 512, EMBED_DIM), jnp.float32), 'value': jax.random.normal(ks[2], (4, 512, EMBED_DIM), jnp.float32), 'Wq': jax.random.uniform(ks[3], (EMBED_DIM, EMBED_DIM), jnp.float32, -s, s), 'bq': jax.random.uniform(ks[4], (EMBED_DIM,), jnp.float32, -s, s), 'Wk': jax.random.uniform(ks[5], (EMBED_DIM, EMBED_DIM), jnp.float32, -s, s), 'bk': jax.random.uniform(ks[6], (EMBED_DIM,), jnp.float32, -s, s), 'Wv': jax.random.uniform(ks[7], (EMBED_DIM, EMBED_DIM), jnp.float32, -s, s), 'bv': jax.random.uniform(ks[8], (EMBED_DIM,), jnp.float32, -s, s), 'Wo': jax.random.uniform(ks[9], (EMBED_DIM, EMBED_DIM), jnp.float32, -s, s), 'bo': jax.random.uniform(ks[10], (EMBED_DIM,), jnp.float32, -s, s)}
        return inp
    _L1_xattn_all = _L1_xattn_setup()
    _L1_xattn_in = {k: v for k, v in _L1_xattn_all.items() if k in ('Wq', 'bq', 'Wk', 'bk', 'Wv', 'bv', 'Wo', 'bo')}
    del _L1_xattn_all

    def _L1_ffn_setup():
        import jax, jax.numpy as jnp
        import numpy as np
        NUM_NOD = 6
        MAX_PREV = 5
        NUM_EDGE = 20
        D = 256
        H = 8
        LN_EPS = 1e-06

        def _layernorm(x, g, b):
            mu = jnp.mean(x, axis=-1, keepdims=True)
            var = jnp.mean(jnp.square(x - mu), axis=-1, keepdims=True)
            return (x - mu) * jax.lax.rsqrt(var + LN_EPS) * g + b

        def _mha(q, k, v, wq, wk, wv, wo):
            B, S, d = q.shape
            dh = d // H
            qh = (q @ wq).reshape(B, S, H, dh)
            kh = (k @ wk).reshape(B, S, H, dh)
            vh = (v @ wv).reshape(B, S, H, dh)
            scores = jnp.einsum('bqhd,bkhd->bhqk', qh, kh) / jnp.sqrt(jnp.asarray(dh, q.dtype))
            attn = jax.nn.softmax(scores, axis=-1)
            ctx = jnp.einsum('bhqk,bkhd->bqhd', attn, vh).reshape(B, S, d)
            return ctx @ wo
        key = jax.random.key(seed)
        ks = jax.random.split(key, 12)
        B, S = (8, 256)
        scale = 1.0 / np.sqrt(D)
        return {'inputs': jax.random.normal(ks[0], (B, S, D), jnp.float32), 'ew': jax.random.uniform(ks[1], (NUM_NOD, 3), jnp.float32), 'act_w': jax.random.uniform(ks[2], (NUM_NOD,), jnp.float32), 'We': jax.random.normal(ks[3], (NUM_EDGE, D, D), jnp.float32) * scale, 'be': jnp.zeros((NUM_EDGE, D), jnp.float32), 'Wq': jax.random.normal(ks[4], (NUM_NOD, D, D), jnp.float32) * scale, 'Wk': jax.random.normal(ks[5], (NUM_NOD, D, D), jnp.float32) * scale, 'Wv': jax.random.normal(ks[6], (NUM_NOD, D, D), jnp.float32) * scale, 'Wo': jax.random.normal(ks[7], (NUM_NOD, D, D), jnp.float32) * scale, 'ln_g': jnp.ones((D,), jnp.float32), 'ln_b': jnp.zeros((D,), jnp.float32)}
    _L1_ffn_all = _L1_ffn_setup()
    _L1_ffn_in = {k: v for k, v in _L1_ffn_all.items() if k in ('ew', 'act_w', 'We', 'be', 'Wq', 'Wk', 'Wv', 'Wo', 'ln_g', 'ln_b')}
    del _L1_ffn_all
    return {'x': x, 'ctx_1024': ctx_1024, 'L0_xattn_Wk': _L0_xattn_in['Wk'], 'L0_xattn_Wv': _L0_xattn_in['Wv'], 'L0_xattn_bv': _L0_xattn_in['bv'], 'L0_xattn_Wq': _L0_xattn_in['Wq'], 'L0_xattn_bq': _L0_xattn_in['bq'], 'L0_xattn_Wo': _L0_xattn_in['Wo'], 'L0_xattn_bo': _L0_xattn_in['bo'], 'L0_ffn_gate_kernel': _L0_ffn_in['gate_kernel'], 'L0_ffn_gate_bias': _L0_ffn_in['gate_bias'], 'L0_ffn_w_gate': _L0_ffn_in['w_gate'], 'L0_ffn_w_up': _L0_ffn_in['w_up'], 'L0_ffn_w_down': _L0_ffn_in['w_down'], 'L0_ffn_sw_gate': _L0_ffn_in['sw_gate'], 'L0_ffn_sw_up': _L0_ffn_in['sw_up'], 'L0_ffn_sw_down': _L0_ffn_in['sw_down'], 'L1_xattn_Wq': _L1_xattn_in['Wq'], 'L1_xattn_bq': _L1_xattn_in['bq'], 'L1_xattn_Wk': _L1_xattn_in['Wk'], 'L1_xattn_bk': _L1_xattn_in['bk'], 'L1_xattn_Wv': _L1_xattn_in['Wv'], 'L1_xattn_bv': _L1_xattn_in['bv'], 'L1_xattn_Wo': _L1_xattn_in['Wo'], 'L1_xattn_bo': _L1_xattn_in['bo'], 'L1_ffn_ew': _L1_ffn_in['ew'], 'L1_ffn_act_w': _L1_ffn_in['act_w'], 'L1_ffn_We': _L1_ffn_in['We'], 'L1_ffn_be': _L1_ffn_in['be'], 'L1_ffn_Wq': _L1_ffn_in['Wq'], 'L1_ffn_Wk': _L1_ffn_in['Wk'], 'L1_ffn_Wv': _L1_ffn_in['Wv'], 'L1_ffn_Wo': _L1_ffn_in['Wo'], 'L1_ffn_ln_g': _L1_ffn_in['ln_g'], 'L1_ffn_ln_b': _L1_ffn_in['ln_b']}

def reference(x, ctx_1024, L0_xattn_Wk, L0_xattn_Wv, L0_xattn_bv, L0_xattn_Wq, L0_xattn_bq, L0_xattn_Wo, L0_xattn_bo, L0_ffn_gate_kernel, L0_ffn_gate_bias, L0_ffn_w_gate, L0_ffn_w_up, L0_ffn_w_down, L0_ffn_sw_gate, L0_ffn_sw_up, L0_ffn_sw_down, L1_xattn_Wq, L1_xattn_bq, L1_xattn_Wk, L1_xattn_bk, L1_xattn_Wv, L1_xattn_bv, L1_xattn_Wo, L1_xattn_bo, L1_ffn_ew, L1_ffn_act_w, L1_ffn_We, L1_ffn_be, L1_ffn_Wq, L1_ffn_Wk, L1_ffn_Wv, L1_ffn_Wo, L1_ffn_ln_g, L1_ffn_ln_b):
    import jax
    import jax.numpy as jnp

    def _L0_xattn_ref(k, v, q, Wk, Wv, bv, Wq, bq, Wo, bo):
        import jax, jax.numpy as jnp
        import numpy as np
        D_MODEL = 256
        B, S = (4, 512)
        kp = jnp.einsum('bsd,ed->bse', k, Wk)
        vp = jnp.einsum('bsd,ed->bse', v, Wv) + bv
        qp = jnp.einsum('bsd,ed->bse', q, Wq) + bq
        scale = 1.0 / jnp.sqrt(jnp.float32(kp.shape[-1]))
        scores = jnp.einsum('bqd,bkd->bqk', qp, kp) * scale
        probs = jax.nn.softmax(scores, axis=-1)
        ctx = jnp.einsum('bqk,bkd->bqd', probs, vp)
        return jnp.einsum('bqd,ed->bqe', ctx, Wo) + bo

    def _L0_ffn_ref(hidden_states, gate_kernel, gate_bias, w_gate, w_up, w_down, sw_gate, sw_up, sw_down):
        import jax, jax.numpy as jnp
        import numpy as np
        H = 256
        M = 128
        E = 16
        TOP_K = 4
        N_GROUP = 4
        TOPK_GROUP = 2
        SCALE = 2.5
        B, S = (2, 256)

        def _gate(x2d, gate_kernel, gate_bias):
            n = x2d.shape[0]
            logits = jnp.dot(x2d.astype(jnp.float32), gate_kernel.astype(jnp.float32))
            scores = jax.nn.sigmoid(logits)
            scores_for_choice = scores + gate_bias
            group_scores = scores_for_choice.reshape(n, N_GROUP, E // N_GROUP)
            top2 = jax.lax.top_k(group_scores, k=2)[0]
            group_sum = jnp.sum(top2, axis=-1)
            group_idx = jax.lax.top_k(group_sum, k=TOPK_GROUP)[1]
            group_mask = jnp.zeros_like(group_sum).at[jnp.arange(n)[:, None], group_idx].set(1.0)
            score_mask = jnp.repeat(group_mask[:, :, None], E // N_GROUP, axis=2).reshape(n, E)
            masked_scores = jnp.where(score_mask > 0, scores_for_choice, 0.0)
            topk_weight, topk_idx = jax.lax.top_k(masked_scores, k=TOP_K)
            topk_weight = topk_weight / (jnp.sum(topk_weight, axis=-1, keepdims=True) + 1e-20)
            topk_weight = topk_weight * SCALE
            return (topk_idx, topk_weight)
        orig_shape = hidden_states.shape
        x = hidden_states.reshape(-1, orig_shape[-1])
        topk_idx, topk_weight = _gate(x, gate_kernel, gate_bias)
        onehot = (topk_idx[:, :, None] == jnp.arange(E)[None, None, :]).astype(topk_weight.dtype)
        combine = jnp.einsum('nke,nk->ne', onehot, topk_weight)
        g = jnp.einsum('nh,ehm->enm', x, w_gate)
        u = jnp.einsum('nh,ehm->enm', x, w_up)
        inter = jax.nn.silu(g) * u
        y_e = jnp.einsum('enm,emh->enh', inter, w_down)
        y = jnp.einsum('ne,enh->nh', combine, y_e)
        shared = jnp.dot(jax.nn.silu(jnp.dot(x, sw_gate)) * jnp.dot(x, sw_up), sw_down)
        return (y + shared).reshape(orig_shape)

    def _L1_xattn_ref(query, key, value, Wq, bq, Wk, bk, Wv, bv, Wo, bo):
        import jax, jax.numpy as jnp
        import numpy as np
        EMBED_DIM = 256
        NUM_HEADS = 16
        HEAD_DIM = EMBED_DIM // NUM_HEADS
        B, T, E = query.shape
        S = key.shape[1]
        H, D = (NUM_HEADS, HEAD_DIM)
        q = (query @ Wq.T + bq).reshape(B, T, H, D).transpose(0, 2, 1, 3)
        k = (key @ Wk.T + bk).reshape(B, S, H, D).transpose(0, 2, 1, 3)
        v = (value @ Wv.T + bv).reshape(B, S, H, D).transpose(0, 2, 1, 3)
        scores = jnp.einsum('bhtd,bhsd->bhts', q, k) / np.sqrt(D)
        causal = jnp.triu(jnp.full((T, S), -jnp.inf, jnp.float32), k=1)
        scores = scores + causal[None, None]
        attn = jax.nn.softmax(scores, axis=-1)
        out = jnp.einsum('bhts,bhsd->bhtd', attn, v)
        out = out.transpose(0, 2, 1, 3).reshape(B, T, E)
        out = out @ Wo.T + bo
        return out

    def _L1_ffn_ref(inputs, ew, act_w, We, be, Wq, Wk, Wv, Wo, ln_g, ln_b):
        import jax, jax.numpy as jnp
        import numpy as np
        NUM_NOD = 6
        MAX_PREV = 5
        NUM_EDGE = 20
        D = 256
        H = 8
        LN_EPS = 1e-06

        def _layernorm(x, g, b):
            mu = jnp.mean(x, axis=-1, keepdims=True)
            var = jnp.mean(jnp.square(x - mu), axis=-1, keepdims=True)
            return (x - mu) * jax.lax.rsqrt(var + LN_EPS) * g + b

        def _mha(q, k, v, wq, wk, wv, wo):
            B, S, d = q.shape
            dh = d // H
            qh = (q @ wq).reshape(B, S, H, dh)
            kh = (k @ wk).reshape(B, S, H, dh)
            vh = (v @ wv).reshape(B, S, H, dh)
            scores = jnp.einsum('bqhd,bkhd->bhqk', qh, kh) / jnp.sqrt(jnp.asarray(dh, q.dtype))
            attn = jax.nn.softmax(scores, axis=-1)
            ctx = jnp.einsum('bhqk,bkhd->bqhd', attn, vh).reshape(B, S, d)
            return ctx @ wo
        nodes = {-1: inputs}
        lind = 0
        for c in range(NUM_NOD):
            nsrc = min(c + 1, MAX_PREV)
            snode = c - nsrc
            eq, ek, ev = (lind + nsrc - 1, lind, lind + nsrc // 2)
            in_q, in_k, in_v = (c - 1, snode, snode + nsrc // 2)
            q = ew[c, 0] * (nodes[in_q] @ We[eq] + be[eq])
            k = ew[c, 1] * (nodes[in_k] @ We[ek] + be[ek])
            v = ew[c, 2] * (nodes[in_v] @ We[ev] + be[ev])
            o = _mha(q, k, v, Wq[c], Wk[c], Wv[c], Wo[c])
            nodes[c] = act_w[c] * o + q
            lind += nsrc
        out = nodes[NUM_NOD - 1]
        return _layernorm(out, ln_g, ln_b)
    x = x + _L0_xattn_ref(ctx_1024, ctx_1024, _layernorm(x, axis=-1), L0_xattn_Wk, L0_xattn_Wv, L0_xattn_bv, L0_xattn_Wq, L0_xattn_bq, L0_xattn_Wo, L0_xattn_bo)
    x = x + _L0_ffn_ref(_layernorm(x, axis=-1), L0_ffn_gate_kernel, L0_ffn_gate_bias, L0_ffn_w_gate, L0_ffn_w_up, L0_ffn_w_down, L0_ffn_sw_gate, L0_ffn_sw_up, L0_ffn_sw_down)
    x = x + _L1_xattn_ref(_layernorm(x, axis=-1), ctx_1024, ctx_1024, L1_xattn_Wq, L1_xattn_bq, L1_xattn_Wk, L1_xattn_bk, L1_xattn_Wv, L1_xattn_bv, L1_xattn_Wo, L1_xattn_bo)
    x = x + _L1_ffn_ref(_layernorm(x, axis=-1), L1_ffn_ew, L1_ffn_act_w, L1_ffn_We, L1_ffn_be, L1_ffn_Wq, L1_ffn_Wk, L1_ffn_Wv, L1_ffn_Wo, L1_ffn_ln_g, L1_ffn_ln_b)
    return x

_drawn_inputs = setup_inputs


def setup_inputs(seed=0):
    import zlib

    import numpy as np

    out = dict(_drawn_inputs(seed))
    spreads = {'L0_xattn_bv': (0.0, 0.1),
     'L0_xattn_bq': (0.0, 0.1),
     'L0_xattn_bo': (0.0, 0.1),
     'L1_ffn_be': (0.0, 0.1),
     'L1_ffn_ln_g': (1.0, 0.2),
     'L1_ffn_ln_b': (0.0, 0.1)}
    factors = {'L1_xattn_Wq': 4.189,
     'L1_xattn_bq': 8.0,
     'L1_xattn_Wk': 4.172,
     'L1_xattn_bk': 200.0,
     'L1_xattn_bv': 5.033,
     'L1_ffn_Wq': 200.0,
     'L1_ffn_Wk': 200.0}
    for name, (base, spread) in spreads.items():
        noise = np.random.default_rng([zlib.crc32(name.encode()), seed]).standard_normal(out[name].shape)
        drawn = base * np.exp(spread * noise) if base else spread * noise
        out[name] = jnp.asarray(drawn.astype(out[name].dtype))
    for name, factor in factors.items():
        out[name] = (out[name] * factor).astype(out[name].dtype)
    return out
```

```python
from contextlib import ExitStack

import concourse.bass as bass
import numpy as np
from concourse import mybir

ALU = mybir.AluOpType
ACT = mybir.ActivationFunctionType
AX = mybir.AxisListType.X
F32 = mybir.dt.float32
I32 = mybir.dt.int32

P = 128
B, S, D = 32, 112, 256
SC = 375
NT, CT = 3, 125
NB = 4
T = NB * S
G = B // NB
DC = D // P
E, M = 16, 128
NG, GE = 4, 4
XH, XD = 16, 16
NODES, PREV = 6, 5
FH, FD = 8, 32
STRIPS = 4
L0_EPS, DAG_EPS = 1e-5, 1e-6
MASKED = -1e30

DAG = []
_at = 0
for _c in range(NODES):
    _n = min(_c + 1, PREV)
    DAG.append(((_c - 1, _at + _n - 1), (_c - _n, _at), (_c - _n + _n // 2, _at + _n // 2)))
    _at += _n

X_SETS = [(c, par, j) for c in range(DC) for par in range(2) for j in range(STRIPS)]
F_SETS = [(c, 0, j) for c in range(DC) for j in range(STRIPS)]



def rows(ap):
    return ap.rearrange("(c p) n -> p c n", p=P)


def build(nc, a, out):
    with ExitStack() as ctx:
        def sb(name, shape, dt=F32):
            return ctx.enter_context(nc.sbuf_tensor(name, shape, dt))

        def sem(name):
            return ctx.enter_context(nc.semaphore(name))

        bank = [ctx.enter_context(nc.psum_tensor(f"bank{i}", [P, 512], F32)) for i in range(8)]
        x2_dram = nc.dram_tensor("x2_scratch", [B * S, D], F32, kind="Internal").ap()

        score0 = sb("score0", [P, DC, D])
        value0 = sb("value0", [P, DC, D])
        gatek = sb("gatek", [P, DC, E])
        w_gate = sb("w_gate", [P, E + 2, DC, M])
        w_up = sb("w_up", [P, E + 2, DC, M])
        w_down = sb("w_down", [P, E + 2, D])
        x_wq, x_wk, x_wv, x_wo = (sb(f"x_w{n}", [P, DC, D]) for n in "qkvo")
        f_edge = sb("f_edge", [P, NODES, DC, D])
        f_wq = sb("f_wq", [P, NODES, DC, D])
        f_kk = sb("f_kk", [P, NODES, DC, D])
        f_vv = sb("f_vv", [P, NODES, DC, D])
        f_wo = sb("f_wo", [P, NODES, DC, D])

        ident = sb("ident", [P, P])
        causal = sb("causal", [S, S])
        earlier = sb("earlier", [S, E * E])
        later_n = sb("later_n", [S, E])
        gbias = sb("gbias", [S, E])
        bias0 = sb("bias0", [S, D])
        bo1 = sb("bo1", [S, D])
        ln_g = sb("ln_g", [S, D])
        ln_b = sb("ln_b", [S, D])
        half_mask = sb("half_mask", [P, 2])
        bq0 = sb("bq0", [P, DC])
        raw_bq0, raw_bv0 = sb("raw_bq0", [P, DC]), sb("raw_bv0", [P, DC])
        bq1, bk1, bv1 = sb("bq1", [P, DC]), sb("bk1", [P, DC]), sb("bv1", [P, DC])
        bk1_half = sb("bk1_half", [P, 2, DC])
        ewc = sb("ewc", [P, NODES, 3])
        actw = sb("actw", [P, NODES])
        be_in = sb("be_in", [P, 3, NODES, DC])
        be_q = sb("be_q", [P, NODES, DC])
        be_kv = sb("be_kv", [P, 2, NODES, DC])

        ARENA = 19000
        arena = sb("arena", [P, ARENA])
        at = [0]

        def cut(*shape):
            n = int(np.prod(shape))
            v = arena[:, at[0]:at[0] + n]
            at[0] += n
            assert at[0] <= ARENA, at[0]
            names = "abcd"[:len(shape)]
            if len(shape) == 1:
                return v
            return v.rearrange(f"p ({' '.join(names)}) -> p {' '.join(names)}", **dict(zip(names, shape)))

        wk0, wq0, wv0, wo0 = cut(DC, D), cut(DC, D), cut(DC, D), cut(DC, D)
        weT = cut(2 * NODES, DC, D)
        wkv = cut(2 * NODES, DC, D)

        at[0] = 0
        xg, xn, x1, xb = cut(NB, D), cut(NB, D), cut(NB, D), cut(NB, D)
        xnT = cut(DC, T)
        ctxg, ctxT = cut(NB, NT, D), cut(DC, NB * SC)
        shared_at = at[0]
        pr0 = cut(NB, SC)
        qT, oT = cut(DC, T), cut(DC, T)
        pT0 = cut(2, NT * S)
        at[0] = shared_at
        sig, choice = cut(NB, E), cut(NB, E)
        pmax, padd = cut(NB * NG, 2), cut(NB * NG, 2)
        gscore = cut(NB * NG)
        gless, glink = cut(NB, NG * NG), cut(NB, NG * NG)
        grank, gback = cut(NB, NG), cut(NB, NG)
        rank, back = cut(NB, E), cut(NB, E)
        comb, csum = cut(NB, E), cut(NB)
        less = cut(NB, E * E)
        combT = cut(T)
        th, inter = cut(2, T), cut(2, T)
        h1, h2 = cut(2, T), cut(2, T)

        at[0] = 0
        yg, x3 = cut(NB, D), cut(NB, D)
        slots_at = at[0]
        node = [cut(DC, T) for _ in range(NODES + 1)]
        kT = cut(2, DC, T)
        qhT, aT = cut(DC, T), cut(DC, T)
        vv = cut(2, NB, D)
        pr, pn, sm = cut(2, NB * S), cut(2, NB * S), cut(2, NB * S)
        SLOTS = 5
        pT = cut(SLOTS, NB * S)
        cT, ynT = node[1], node[2]
        at[0] = slots_at + 4 * DC * T
        yn = cut(NB, D)

        stats = sb("stats", [S, NB, 6])
        mv = sb("mv", [S, NB, 2])
        rs_v, rs_y, rs_t = sb("rs_v", [S, NB]), sb("rs_y", [S, NB]), sb("rs_t", [S, NB])
        RING = 8
        nmax, nbias = sb("nmax", [S, RING, NB]), sb("nbias", [S, RING, NB])
        rsum, rinv = sb("rsum", [S, RING, NB]), sb("rinv", [S, RING, NB])

        setup_loaded = sem("setup_loaded")
        fused = sem("fused")
        fused_copied = sem("fused_copied")
        loaded = sem("loaded")
        inputs_used = sem("inputs_used")
        vec = sem("vec")
        norm_ready = sem("norm_ready")
        turned = sem("turned")
        xnT_ready = sem("xnT_ready")
        q_ps, q_ready = sem("q_ps"), sem("q_ready")
        s_ps, max_ready = sem("s_ps"), sem("max_ready")
        masked = sem("masked")
        exp_done = sem("exp_done")
        t_ps, t_copied = sem("t_ps"), sem("t_copied")
        o_ps, o_ready = sem("o_ps"), sem("o_ready")
        out_ps = sem("out_ps")
        bias_added = sem("bias_added")
        logit_ps, sig_ready = sem("logit_ps"), sem("sig_ready")
        comb_ready, combT_ps, combT_ready = sem("comb_ready"), sem("combT_ps"), sem("combT_ready")
        gu_ps, th_ready = sem("gu_ps"), sem("th_ready")
        h1_done, h2_done = sem("h1_done"), sem("h2_done")
        cb_ps, inter_ready, down_ps = sem("cb_ps"), sem("inter_ready"), sem("down_ps")
        k_ps, k_ready = sem("k_ps"), sem("k_ready")
        v_ps, v_ready, v_zero = sem("v_ps"), sem("v_ready"), sem("v_zero")
        e_ps, e_ready = sem("e_ps"), sem("e_ready")
        rinv_ready, normed = sem("rinv_ready"), sem("normed")
        node_ready = sem("node_ready")
        fin_ps = sem("fin_ps")
        result = sem("result")
        stored = sem("stored")
        go_pe, go_act, go_dve, go_pool = sem("go_pe"), sem("go_act"), sem("go_dve"), sem("go_pool")
        per_iteration = [
            setup_loaded, fused, fused_copied, loaded, inputs_used, vec, norm_ready, turned, xnT_ready,
            q_ps, q_ready, s_ps, max_ready, masked, exp_done, t_ps, t_copied, o_ps, o_ready, out_ps,
            bias_added, logit_ps, sig_ready, comb_ready, combT_ps, combT_ready, gu_ps, th_ready, h1_done,
            h2_done, cb_ps, inter_ready, down_ps, k_ps, k_ready, v_ps, v_ready, v_zero, e_ps, e_ready,
            rinv_ready, normed, node_ready, fin_ps, result, stored,
        ]
        counts = {}
        block = ctx.enter_context(nc.Block())

        def heads(sets, base, mask):
            return [(base + i, *s) for i, s in enumerate(sets)]

        X = heads(X_SETS, 0, True)
        F = [heads(F_SETS, len(X_SETS) + c * len(F_SETS), False) for c in range(NODES)]
        NX = len(X_SETS) // STRIPS
        NF = len(F_SETS) // STRIPS

        @block.sync
        def _(sp):
            def release():
                for s in per_iteration:
                    sp.sem_clear(s)
                for s in (go_pe, go_act, go_dve, go_pool):
                    sp.sem_inc(s, 1)

            n = [0]

            def load(dst, src):
                n[0] += 16
                sp.dma_start(dst, src).then_inc(setup_loaded, 16)

            load(wq0[:], rows(a["L0_xattn_Wq"]))
            load(wk0[:], rows(a["L0_xattn_Wk"]))
            load(wv0[:], rows(a["L0_xattn_Wv"]))
            load(wo0[:], rows(a["L0_xattn_WoT"]))
            for i in range(NODES):
                load(weT[:, i], rows(a["L1_ffn_WeT"][DAG[i][1][1]]))
                load(weT[:, NODES + i], rows(a["L1_ffn_WeT"][DAG[i][2][1]]))
                load(f_edge[:, i], rows(a["L1_ffn_We"][DAG[i][0][1]]))
                load(wkv[:, i], rows(a["L1_ffn_Wk"][i]))
                load(wkv[:, NODES + i], rows(a["L1_ffn_Wv"][i]))
                load(f_wq[:, i], rows(a["L1_ffn_Wq"][i]))
                load(f_wo[:, i], rows(a["L1_ffn_Wo"][i]))
            load(x_wq[:], rows(a["L1_xattn_WqT"]))
            load(x_wk[:], rows(a["L1_xattn_WkT"]))
            load(x_wv[:], rows(a["L1_xattn_WvT"]))
            load(x_wo[:], rows(a["L1_xattn_WoT"]))
            load(gatek[:], rows(a["L0_ffn_gate_kernel"]))
            for c in range(DC):
                load(w_gate[:, 2:, c], a["L0_ffn_w_gate"][:, c * P:(c + 1) * P, :].rearrange("e p m -> p e m"))
                load(w_up[:, 2:, c], a["L0_ffn_w_up"][:, c * P:(c + 1) * P, :].rearrange("e p m -> p e m"))
                load(w_gate[:, 0:2, c], a["L0_ffn_sw_gate"][c * P:(c + 1) * P, :].rearrange("p (e m) -> p e m", m=M))
                load(w_up[:, 0:2, c], a["L0_ffn_sw_up"][c * P:(c + 1) * P, :].rearrange("p (e m) -> p e m", m=M))
            load(w_down[:, 2:], a["L0_ffn_w_down"].rearrange("e p n -> p e n"))
            load(w_down[:, 0:2], rows(a["L0_ffn_sw_down"]))
            load(ident[:], a["c_ident"])
            load(causal[:], a["c_causal"])
            load(half_mask[:], a["c_half_mask"])

            def to_all(dst, src):
                load(dst, src.partition_broadcast(dst.shape[0]))

            to_all(earlier[:], a["c_earlier"])
            to_all(later_n[:], a["c_later_n"])
            to_all(gbias[:], a["L0_ffn_gate_bias"])
            to_all(bias0[:], a["L0_xattn_bo"])
            to_all(bo1[:], a["L1_xattn_bo"])
            to_all(ln_g[:], a["L1_ffn_ln_g"])
            to_all(ln_b[:], a["L1_ffn_ln_b"])
            to_all(ewc[:].rearrange("p n k -> p (n k)"), a["L1_ffn_ew"].rearrange("n k -> (n k)"))
            to_all(actw[:], a["L1_ffn_act_w"])
            for dst, name in ((raw_bq0, "L0_xattn_bq"), (raw_bv0, "L0_xattn_bv"), (bq1, "L1_xattn_bq"),
                              (bk1, "L1_xattn_bk"), (bv1, "L1_xattn_bv")):
                load(dst[:], a[name])
            for i in range(NODES):
                for k in range(3):
                    load(be_in[:, k, i], a["L1_ffn_beT"][DAG[i][k][1]])
            sp.wait_ge(setup_loaded, n[0])
            counts["setup"] = n[0]

            def load_group(g):
                sp.dma_start(xg[0:S], a["x"][bass.ds(g * T, T), :].rearrange("(b s) d -> s b d", s=S)).then_inc(loaded, 16)
                for b in range(NB):
                    sp.dma_start(ctxg[0:CT, b], a["ctx"][bass.ds((g * NB + b) * SC, SC), :].rearrange(
                        "(t p) d -> p t d", p=CT)).then_inc(loaded, 16)
                sp.dma_start(ctxT[:], a["ctxT"][:, bass.ds(g * NB * SC, NB * SC)].rearrange(
                    "(c p) s -> p c s", p=P)).then_inc(loaded, 16)

            def store_group(g, dst, src):
                sp.wait_ge(result, 2)
                sp.dma_start(dst[bass.ds(g * T, T), :].rearrange("(b s) d -> s b d", s=S), src[0:S]).then_inc(stored, 16)
                sp.wait_ge(stored, 16)

            LOADS = 16 * (2 + NB)
            sp.wait_ge(result, 1)
            load_group(0)
            sp.wait_ge(loaded, LOADS)
            release()
            with sp.Fori(0, G - 1) as g:
                sp.wait_ge(inputs_used, 1)
                load_group(g + 1)
                store_group(g, x2_dram, xn)
                sp.wait_ge(loaded, LOADS)
                release()
            store_group(G - 1, x2_dram, xn)

            def load_group2(g):
                sp.dma_start(yg[0:S], x2_dram[bass.ds(g * T, T), :].rearrange("(b s) d -> s b d", s=S)).then_inc(loaded, 16)
                for c in range(DC):
                    sp.dma_start(cT[:, c].rearrange("p (b s) -> p b s", b=NB),
                                 a["ctxT"][c * P:(c + 1) * P, bass.ds(g * NB * SC, NB * SC)].rearrange(
                                     "p (b s) -> p b s", b=NB)[:, :, 0:S]).then_inc(loaded, 16)

            load_group2(0)
            sp.wait_ge(loaded, 48)
            release()
            with sp.Fori(0, G - 1) as g:
                store_group(g, out, x3)
                load_group2(g + 1)
                sp.wait_ge(loaded, 48)
                release()
            store_group(G - 1, out, x3)

        @block.tensor
        def _(pe):
            mm = nc.tensor.matmul

            pe.wait_ge(setup_loaded, counts["setup"])
            jobs = [(wq0, wk0), (wv0, wo0)] + [(weT[:, i], wkv[:, i]) for i in range(2 * NODES)]
            for i, (lhsT, rhs) in enumerate(jobs):
                if i >= 8:
                    pe.wait_ge(fused_copied, i - 7)
                for o in range(DC):
                    for c in range(DC):
                        last = mm(bank[i % 8][:, o * D:(o + 1) * D], lhsT[:, c, o * P:(o + 1) * P], rhs[:, c, :],
                                  start=(c == 0), stop=(c == DC - 1))
                last.then_inc(fused, 1)
            i = len(jobs)
            pe.wait_ge(fused_copied, i - 7)
            for o in range(DC):
                for c in range(DC):
                    mm(bank[i % 8][:, o:o + 1], wk0[:, c, o * P:(o + 1) * P], raw_bq0[:, c:c + 1],
                       start=(c == 0), stop=(c == DC - 1))
            for k in range(2 * NODES):
                for o in range(DC):
                    for c in range(DC):
                        last = mm(bank[i % 8][:, 2 + 2 * k + o:3 + 2 * k + o], wkv[:, k, c, o * P:(o + 1) * P],
                                  be_in[:, 1 + k // NODES, k % NODES, c:c + 1], start=(c == 0), stop=(c == DC - 1))
            last.then_inc(fused, 1)
            i += 1
            pe.wait_ge(fused_copied, i - 7)
            for c in range(DC):
                last = mm(bank[i % 8][0:S, 0:D], raw_bv0[:, c:c + 1].to_broadcast([P, S]), wo0[:, c, :],
                          start=(c == 0), stop=(c == DC - 1))
            last.then_inc(fused, 1)

            def go():
                pe.wait_ge(go_pe, 1)
                pe.sem_clear(go_pe)

            def turn(k):
                for b in range(NB):
                    pe.wait_ge(norm_ready, NB * k + b + 1)
                    for c in range(DC):
                        src = (xn if phase == 1 else yn)[0:S, b, c * P:(c + 1) * P]
                        last = nc.tensor.transpose(bank[c][:, b * S:(b + 1) * S], src, ident[0:S, 0:S])
                last.then_inc(turned, 1)

            def project(bank0, w, xT, done):
                for o in range(DC):
                    for c in range(DC):
                        last = mm(bank[bank0 + o][:, 0:T], w[:, c, o * P:(o + 1) * P], xT[:, c, :],
                                  start=(c == 0), stop=(c == DC - 1))
                    last.then_inc(done, 1)

            def project_tokens(bank0, xT, w, done):
                for b in range(NB):
                    for c in range(DC):
                        last = mm(bank[bank0 + b // 2][0:S, (b % 2) * D:(b % 2 + 1) * D],
                                  xT[:, c, b * S:(b + 1) * S], w[:, c, :], start=(c == 0), stop=(c == DC - 1))
                    if b % 2:
                        last.then_inc(done, 1)

            phase = 1
            with pe.Fori(0, G):
                go()
                turn(0)
                pe.wait_ge(xnT_ready, DC)
                project(2, score0, xnT, q_ps)
                pe.wait_ge(q_ready, DC)
                for b in range(NB):
                    for c in range(DC):
                        last = mm(bank[4 + b][0:S, 0:SC], qT[:, c, b * S:(b + 1) * S],
                                  ctxT[:, c, b * SC:(b + 1) * SC], start=(c == 0), stop=(c == DC - 1))
                    last.then_inc(s_ps, 1)
                for i in range(NB + 1):
                    if i < NB:
                        pe.wait_ge(exp_done, i + 1)
                        if i >= 2:
                            pe.wait_ge(t_copied, i - 1)
                        for t in range(NT):
                            last = nc.tensor.transpose(bank[i % 2][0:CT, t * S:(t + 1) * S],
                                                       pr0[0:S, i, t * CT:(t + 1) * CT], ident[0:S, 0:S])
                        last.then_inc(t_ps, 1)
                    if i >= 1:
                        b = i - 1
                        pe.wait_ge(t_copied, b + 1)
                        for c in range(DC):
                            for t in range(NT):
                                last = mm(bank[2 + c][:, b * S:(b + 1) * S], ctxg[0:CT, b, t, c * P:(c + 1) * P],
                                          pT0[0:CT, b % 2, t * S:(t + 1) * S], start=(t == 0), stop=(t == NT - 1))
                        last.then_inc(o_ps, 1)
                pe.wait_ge(o_ready, DC)
                project_tokens(0, oT, value0, out_ps)
                turn(1)
                pe.wait_ge(xnT_ready, 2 * DC)
                for b in range(NB):
                    for c in range(DC):
                        last = mm(bank[2][0:S, b * E:(b + 1) * E], xnT[:, c, b * S:(b + 1) * S], gatek[:, c, :],
                                  start=(c == 0), stop=(c == DC - 1))
                last.then_inc(logit_ps, 1)
                for k in range(E + 3):
                    if k < E + 2:
                        if k >= 4:
                            pe.wait_ge(h2_done, k - 3)
                        elif k >= 2:
                            pe.wait_ge(inter_ready, k - 1)
                        for w, bk in ((w_gate, 4), (w_up, 6)):
                            for c in range(DC):
                                last = mm(bank[bk + k % 2][:, 0:T], w[:, k, c, :], xnT[:, c, :],
                                          start=(c == 0), stop=(c == DC - 1))
                        last.then_inc(gu_ps, 1)
                    if k == 1:
                        pe.wait_ge(comb_ready, 1)
                        for b in range(NB):
                            last = nc.tensor.transpose(bank[3][0:E, b * S:(b + 1) * S], comb[0:S, b, :], ident[0:S, 0:S])
                        last.then_inc(combT_ps, 1)
                    if 2 <= k < E + 2:
                        pe.wait_ge(combT_ready, 1)
                        if k >= 4:
                            pe.wait_ge(inter_ready, k - 1)
                        mm(bank[2 + k % 2][:, 0:T], ident[0:E, k - 2:k - 1].to_broadcast([E, P]), combT[0:E, :],
                           start=True, stop=True).then_inc(cb_ps, 1)
                    if k >= 1:
                        pe.wait_ge(inter_ready, k)
                        for b in range(NB):
                            last = mm(bank[b // 2][0:S, (b % 2) * D:(b % 2 + 1) * D],
                                      inter[:, (k - 1) % 2, b * S:(b + 1) * S], w_down[:, k - 1, :],
                                      start=(k == 1 and b % 2 == 0), stop=(k == E + 2), skip_group_check=True)
                        last.then_inc(down_ps, 1)

            def attend(sets, cross):
                first = sets[0][0]
                for i in range(len(sets) + 4):
                    if i < len(sets):
                        n, c, par, j = sets[i]
                        if i >= 4:
                            pe.wait_ge(masked if cross else exp_done, n - 3)
                        rows_ = slice(32 * j, 32 * j + 32)
                        for b in range(NB):
                            last = mm(bank[j][0:S, b * S:(b + 1) * S], qhT[rows_, c, b * S:(b + 1) * S],
                                      kT[rows_, par, c, b * S:(b + 1) * S], start=True, stop=True)
                        last.then_inc(s_ps, 1)
                    if 0 <= i - 3 < len(sets):
                        n = first + i - 3
                        pe.wait_ge(normed, n + 1)
                        if n >= 2:
                            pe.wait_ge(t_copied, n - 1)
                        for b in range(NB):
                            last = nc.tensor.transpose(bank[4 + n % 2][0:S, b * S:(b + 1) * S],
                                                       pn[0:S, n % 2, b * S:(b + 1) * S], ident[0:S, 0:S])
                        last.then_inc(t_ps, 1)
                    if i >= 7 and (i - 4) % STRIPS == STRIPS - 1:
                        n, c, par, _ = sets[i - 4]
                        pe.wait_ge(t_copied, n + 1)
                        for b in range(NB):
                            for j in range(STRIPS):
                                at_ = n - (STRIPS - 1) + j
                                col = c * P + 32 * j
                                last = mm(bank[6 + c][32 * j:32 * j + 32, b * S:(b + 1) * S],
                                          vv[0:S, par, b, col:col + 32], pT[0:S, at_ % SLOTS, b * S:(b + 1) * S],
                                          start=(not cross or (par == 0 and b == 0)), stop=(not cross or par == 1),
                                          skip_group_check=True)
                        last.then_inc(o_ps, 1)

            phase = 2
            with pe.Fori(0, G):
                go()
                project(2, x_wk, cT, k_ps)
                project_tokens(4, cT, x_wv, v_ps)
                turn(0)
                pe.wait_ge(xnT_ready, DC)
                project(6, x_wq, ynT, q_ps)
                pe.wait_ge(q_ready, DC)
                pe.wait_ge(k_ready, 2 * DC)
                pe.wait_ge(v_ready, 4)
                attend(X, True)
                pe.wait_ge(o_ready, DC)
                project_tokens(0, aT, x_wo, out_ps)
                turn(1)
                pe.wait_ge(xnT_ready, 2 * DC)
                for c in range(NODES):
                    (nq, _), (nk, _), (nv, _) = DAG[c]
                    if c:
                        pe.wait_ge(node_ready, DC * c)
                    project(6, f_edge[:, c], node[nq + 1], e_ps)
                    project(2, f_kk[:, c], node[nk + 1], k_ps)
                    project_tokens(4, node[nv + 1], f_vv[:, c], v_ps)
                    pe.wait_ge(e_ready, DC * (c + 1))
                    project(0, f_wq[:, c], node[c + 1], q_ps)
                    pe.wait_ge(q_ready, DC * (c + 2))
                    pe.wait_ge(k_ready, 2 * DC + DC * (c + 1))
                    pe.wait_ge(v_ready, 4 + 2 * (c + 1))
                    attend(F[c], False)
                    pe.wait_ge(o_ready, DC * (c + 2))
                    project(0, f_wo[:, c], aT, out_ps)
                pe.wait_ge(node_ready, DC * NODES)
                for b in range(NB):
                    for c in range(DC):
                        last = nc.tensor.transpose(bank[2 + b // 2][0:S, (b % 2) * D + c * P:(b % 2) * D + (c + 1) * P],
                                                   node[NODES][:, c, b * S:(b + 1) * S], ident[:, :])
                    if b % 2:
                        last.then_inc(fin_ps, 1)

        @block.scalar
        def _(act):
            def go():
                act.wait_ge(go_act, 1)
                act.sem_clear(go_act)

            def take_turned(k, dst):
                act.wait_ge(turned, k + 1)
                for c in range(DC):
                    nc.scalar.activation(dst[:, c, :], bank[c][:, 0:T], ACT.Identity).then_inc(xnT_ready, 1)

            with act.Fori(0, G):
                go()
                take_turned(0, xnT)
                for o in range(DC):
                    act.wait_ge(q_ps, o + 1)
                    nc.scalar.activation(qT[:, o, :], bank[2 + o][:, 0:T], ACT.Identity,
                                         bias=bq0[:, o:o + 1]).then_inc(q_ready, 1)
                for b in range(NB):
                    act.wait_ge(max_ready, b + 1)
                    nc.scalar.activation(pr0[0:S, b, :], bank[4 + b][0:S, 0:SC], ACT.Exp, bias=nbias[:, 0, b:b + 1],
                                         scale=float(D) ** -0.5, accum_out=rsum[:, 0, b:b + 1]).then_inc(exp_done, 1)
                act.wait_ge(o_ps, NB)
                for c in range(DC):
                    nc.scalar.activation(oT[:, c, :], bank[2 + c][:, 0:T], ACT.Identity).then_inc(o_ready, 1)
                take_turned(1, xnT)
                act.wait_ge(logit_ps, 1)
                nc.scalar.activation(sig[0:S], bank[2][0:S, 0:NB * E].rearrange("p (b e) -> p b e", b=NB),
                                     ACT.Tanh, scale=0.5).then_inc(sig_ready, 1)
                for k in range(E + 2):
                    act.wait_ge(gu_ps, k + 1)
                    if k >= 2:
                        act.wait_ge(h1_done, k - 1)
                    nc.scalar.activation(th[:, k % 2, :], bank[4 + k % 2][:, 0:T], ACT.Tanh,
                                         scale=0.5).then_inc(th_ready, 1)

            def attend(sets, cross, biases, rounds0, chunks0):
                per_chunk = 2 if cross else 1

                def evacuate(c):
                    act.wait_ge(o_ps, rounds0 + per_chunk * (c + 1))
                    nc.scalar.activation(aT[:, c, :], bank[6 + c][:, 0:T], ACT.Identity,
                                         bias=biases[:, c:c + 1]).then_inc(o_ready, 1)

                scale = float(XD if cross else FD) ** -0.5
                for i, (n, _, _, j) in enumerate(sets):
                    act.wait_ge(max_ready, n + 1)
                    if n >= 2:
                        act.wait_ge(normed, n - 1)
                    for b in range(NB):
                        src = sm[0:S, n % 2, b * S:(b + 1) * S] if cross else bank[j][0:S, b * S:(b + 1) * S]
                        last = nc.scalar.activation(pr[0:S, n % 2, b * S:(b + 1) * S], src, ACT.Exp,
                                                    bias=nbias[:, n % RING, b:b + 1], scale=scale,
                                                    accum_out=rsum[:, n % RING, b:b + 1])
                    last.then_inc(exp_done, 1)
                    if i == STRIPS * per_chunk + 3:
                        evacuate(0)
                evacuate(1)

            with act.Fori(0, G):
                go()
                for o in range(DC):
                    act.wait_ge(k_ps, o + 1)
                    for par in range(2):
                        nc.scalar.activation(kT[:, par, o, :], bank[2 + o][:, 0:T], ACT.Identity,
                                             scale=half_mask[:, par:par + 1],
                                             bias=bk1_half[:, par, o:o + 1]).then_inc(k_ready, 1)
                take_turned(0, ynT)
                for o in range(DC):
                    act.wait_ge(q_ps, o + 1)
                    nc.scalar.activation(qhT[:, o, :], bank[6 + o][:, 0:T], ACT.Identity,
                                         bias=bq1[:, o:o + 1]).then_inc(q_ready, 1)
                attend(X, True, bv1, 0, 0)
                take_turned(1, node[0])
                for c in range(NODES):
                    for o in range(DC):
                        act.wait_ge(k_ps, DC * (c + 1) + o + 1)
                        nc.scalar.activation(kT[:, 0, o, :], bank[2 + o][:, 0:T], ACT.Identity,
                                             scale=ewc[:, c, 1:2], bias=be_kv[:, 0, c, o:o + 1]).then_inc(k_ready, 1)
                    for o in range(DC):
                        act.wait_ge(q_ps, DC * (c + 1) + o + 1)
                        nc.scalar.activation(qhT[:, o, :], bank[o][:, 0:T], ACT.Identity).then_inc(q_ready, 1)
                    attend(F[c], False, be_kv[:, 1, c], NX + NF * c, 0)

        @block.vector
        def _(dve):
            V = nc.vector
            chain = [0]

            def link(ins):
                chain[0] += 1
                ins.then_inc(vec, 1)
                dve.wait_ge(vec, chain[0])

            def go():
                dve.wait_ge(go_dve, 1)
                dve.sem_clear(go_dve)
                chain[0] = 0

            def layernorm(dst, src, eps, k):
                if k:
                    dve.wait_ge(norm_ready, NB * k)
                for b in range(NB):
                    last = V.bn_stats(stats[:, b, :], src[0:S, b, :])
                link(last)
                for b in range(NB):
                    last = V.bn_aggr(mv[:, b, :], stats[:, b, :])
                link(last)
                link(V.tensor_scalar(rs_v[:], mv[:, :, 1], eps, None, ALU.add))
                link(V.tensor_single_scalar(rs_y[:].bitcast(I32), rs_v[:].bitcast(I32), 1, ALU.arith_shift_right))
                link(V.tensor_scalar(rs_y[:].bitcast(I32), rs_y[:].bitcast(I32), -1.0, float(0x5F3759DF), ALU.mult, ALU.add))
                for _ in range(4):
                    link(V.tensor_tensor(rs_t[:], rs_v[:], rs_y[:], ALU.mult))
                    link(V.scalar_tensor_tensor(rs_t[:], rs_t[:], -0.5, rs_y[:], ALU.mult, ALU.mult))
                    link(V.scalar_tensor_tensor(rs_y[:], rs_t[:], 1.5, rs_y[:], ALU.add, ALU.mult))
                for b in range(NB):
                    V.tensor_scalar(dst[0:S, b, :], src[0:S, b, :], mv[:, b, 0:1], rs_y[:, b:b + 1],
                                    ALU.subtract, ALU.mult).then_inc(norm_ready, 1)

            dve.wait_ge(setup_loaded, counts["setup"])
            for par in range(2):
                V.tensor_scalar(bk1_half[:, par, :], bk1[:], half_mask[:, par:par + 1], None, ALU.mult)
            V.tensor_tensor(be_q[:], be_in[:, 0], ewc[:, :, 0:1].to_broadcast([P, NODES, DC]), ALU.mult)
            dsts = [score0[:], value0[:]] + [f_kk[:, i] for i in range(NODES)] + [f_vv[:, i] for i in range(NODES)]
            for i, dst in enumerate(dsts):
                dve.wait_ge(fused, i + 1)
                V.tensor_copy(dst, bank[i % 8][:, :].rearrange("p (c n) -> p c n", c=DC)).then_inc(fused_copied, 1)
            i = len(dsts)
            dve.wait_ge(fused, i + 1)
            V.tensor_copy(bq0[:], bank[i % 8][:, 0:DC])
            for k in range(2):
                last = V.tensor_tensor(be_kv[:, k], bank[i % 8][:, 2 + k * NODES * DC:2 + (k + 1) * NODES * DC].rearrange(
                    "p (n c) -> p n c", c=DC), ewc[:, :, 1 + k:2 + k].to_broadcast([P, NODES, DC]), ALU.mult)
            last.then_inc(fused_copied, 1)
            dve.wait_ge(fused, i + 2)
            V.tensor_tensor(bias0[:], bank[(i + 1) % 8][0:S, 0:D], bias0[:], ALU.add).then_inc(result, 1)

            def route():
                s64 = choice[0:S]
                link(V.tensor_scalar(s64, sig[0:S], 0.5, 0.5, ALU.mult, ALU.add))
                link(V.tensor_tensor(s64, s64, gbias[:].unsqueeze(1).to_broadcast([S, NB, E]), ALU.add))
                quads = s64.rearrange("p b (g h w) -> p (b g) h w", g=NG, h=2)
                V.tensor_tensor(pmax[0:S], quads[:, :, :, 0], quads[:, :, :, 1], ALU.max)
                link(V.tensor_tensor(padd[0:S], quads[:, :, :, 0], quads[:, :, :, 1], ALU.add))
                link(V.tensor_tensor(gscore[0:S], pmax[0:S, :, 0], pmax[0:S, :, 1], ALU.add))
                for h in range(2):
                    link(V.tensor_tensor(gscore[0:S], gscore[0:S], padd[0:S, :, h], ALU.max))

                def ranks(v, n, less_, rank_, back_):
                    sq = [S, NB, n, n]
                    L = less_[0:S].rearrange("p b (i j) -> p b i j", i=n)
                    for b in range(NB):
                        last_ = V.tensor_tensor(L[:, b], v[:, b, :].unsqueeze(1).to_broadcast([S, n, n]),
                                                v[:, b, :].unsqueeze(2).to_broadcast([S, n, n]), ALU.is_ge)
                    link(last_)
                    e_ = earlier[:].rearrange("p (i j) -> p i j", i=E)[:, 0:n, 0:n]
                    for b in range(NB):
                        last_ = V.tensor_tensor(L[:, b], L[:, b], e_, ALU.mult)
                    link(last_)
                    V.tensor_reduce(rank_[0:S], L, axis=AX, op=ALU.add)
                    link(V.tensor_reduce(back_[0:S], L.rearrange("p b i j -> p b j i"), axis=AX, op=ALU.add))
                    link(V.tensor_tensor(rank_[0:S], rank_[0:S], back_[0:S], ALU.subtract))
                    link(V.tensor_tensor(rank_[0:S], rank_[0:S],
                                         later_n[:, E - n:E].unsqueeze(1).to_broadcast([S, NB, n]), ALU.add))

                ranks(gscore[0:S].rearrange("p (b g) -> p b g", b=NB), NG, gless, grank, gback)
                link(V.tensor_single_scalar(grank[0:S], grank[0:S], 1.5, ALU.is_lt))
                link(V.tensor_tensor(s64.rearrange("p b (g w) -> p (b g) w", g=NG), s64.rearrange("p b (g w) -> p (b g) w", g=NG),
                                     grank[0:S].rearrange("p b g -> p (b g)").unsqueeze(2).to_broadcast([S, NB * NG, GE]), ALU.mult))
                ranks(s64, E, less, rank, back)
                link(V.scalar_tensor_tensor(comb[0:S], rank[0:S], 3.5, s64, ALU.is_lt, ALU.mult))
                link(V.tensor_reduce(csum[0:S], comb[0:S], axis=AX, op=ALU.add))
                link(V.tensor_scalar(csum[0:S], csum[0:S], 1e-20, None, ALU.add))
                link(V.reciprocal(csum[0:S], csum[0:S]))
                V.scalar_tensor_tensor(comb[0:S], comb[0:S], 2.5, csum[0:S].unsqueeze(2).to_broadcast([S, NB, E]),
                                       ALU.mult, ALU.mult).then_inc(comb_ready, 1)

            with dve.Fori(0, G):
                go()
                layernorm(xn, xg, L0_EPS, 0)
                for b in range(NB):
                    dve.wait_ge(s_ps, b + 1)
                    link(V.tensor_reduce(nmax[:, 0, b:b + 1], bank[4 + b][0:S, 0:SC], axis=AX, op=ALU.max))
                    V.tensor_scalar(nbias[:, 0, b:b + 1], nmax[:, 0, b:b + 1], -float(D) ** -0.5, None,
                                    ALU.mult).then_inc(max_ready, 1)
                for b in range(NB):
                    dve.wait_ge(t_ps, b + 1)
                    if b >= 2:
                        dve.wait_ge(o_ps, b - 1)
                    V.tensor_copy(pT0[0:CT, b % 2, :], bank[b % 2][0:CT, 0:NT * S]).then_inc(t_copied, 1)
                dve.wait_ge(exp_done, NB)
                link(V.reciprocal(rinv[:, 0, :], rsum[:, 0, :]))
                dve.wait_ge(bias_added, 1)
                for b in range(NB):
                    dve.wait_ge(out_ps, b // 2 + 1)
                    last = V.scalar_tensor_tensor(x1[0:S, b, :], bank[b // 2][0:S, (b % 2) * D:(b % 2 + 1) * D],
                                                  rinv[:, 0, b:b + 1], xb[0:S, b, :], ALU.mult, ALU.add)
                last.then_inc(inputs_used, 1)
                dve.wait_ge(inputs_used, 1)
                layernorm(xn, x1, L0_EPS, 1)
                dve.wait_ge(sig_ready, 1)
                route()
                for k in range(E + 2):
                    dve.wait_ge(th_ready, k + 1)
                    if k >= 2:
                        dve.wait_ge(inter_ready, k - 1)
                    V.scalar_tensor_tensor(h1[:, k % 2, :], th[:, k % 2, :], 1.0, bank[4 + k % 2][:, 0:T],
                                           ALU.add, ALU.mult).then_inc(h1_done, 1)
                    dve.wait_ge(h1_done, k + 1)
                    if k >= 2:
                        dve.wait_ge(down_ps, k - 1)
                    if k < 2:
                        V.scalar_tensor_tensor(inter[:, k % 2, :], h1[:, k % 2, :], 0.5, bank[6 + k % 2][:, 0:T],
                                               ALU.mult, ALU.mult).then_inc(inter_ready, 1)
                    else:
                        V.scalar_tensor_tensor(h2[:, k % 2, :], h1[:, k % 2, :], 0.5, bank[6 + k % 2][:, 0:T],
                                               ALU.mult, ALU.mult).then_inc(h2_done, 1)
                        dve.wait_ge(h2_done, k - 1)
                        dve.wait_ge(cb_ps, k - 1)
                        V.tensor_tensor(inter[:, k % 2, :], h2[:, k % 2, :], bank[2 + k % 2][:, 0:T], ALU.mult).then_inc(inter_ready, 1)
                    if k == 0:
                        dve.wait_ge(combT_ps, 1)
                        V.tensor_copy(combT[0:E, :], bank[3][0:E, 0:T]).then_inc(combT_ready, 1)
                dve.wait_ge(down_ps, E + 2)
                for h in range(2):
                    V.tensor_tensor(xn[0:S, 2 * h:2 * h + 2, :], bank[h][0:S, :].rearrange("p (b d) -> p b d", b=2),
                                    x1[0:S, 2 * h:2 * h + 2, :], ALU.add).then_inc(result, 1)

            def attend(sets, cross):
                scale = float(XD if cross else FD) ** -0.5
                first = sets[0][0]
                for i in range(len(sets) + 3):
                    if i < len(sets):
                        n, _, _, j = sets[i]
                        dve.wait_ge(s_ps, n + 1)
                        if n >= RING:
                            dve.wait_ge(max_ready, n - RING + 1)
                        src = bank[j][0:S, 0:T].rearrange("p (b s) -> p b s", b=NB)
                        if cross:
                            if n >= 2:
                                dve.wait_ge(exp_done, n - 1)
                            smv = sm[0:S, n % 2, :].rearrange("p (b s) -> p b s", b=NB)
                            V.tensor_tensor(smv, src, causal[:].unsqueeze(1).to_broadcast([S, NB, S]),
                                            ALU.add).then_inc(masked, 1)
                            dve.wait_ge(masked, n + 1)
                            src = smv
                        link(V.tensor_reduce(nmax[:, n % RING, :], src, axis=AX, op=ALU.max))
                        V.tensor_scalar(nbias[:, n % RING, :], nmax[:, n % RING, :], -scale, None,
                                        ALU.mult).then_inc(max_ready, 1)
                    if 0 <= i - 1 < len(sets):
                        n = first + i - 1
                        dve.wait_ge(exp_done, n + 1)
                        if n >= RING:
                            dve.wait_ge(normed, n - RING + 1)
                        V.reciprocal(rinv[:, n % RING, :], rsum[:, n % RING, :]).then_inc(rinv_ready, 1)
                    if 0 <= i - 3 < len(sets):
                        n = first + i - 3
                        dve.wait_ge(t_ps, n + 1)
                        if n >= SLOTS:
                            dve.wait_ge(o_ps, (n - SLOTS) // STRIPS + 1)
                        V.tensor_copy(pT[0:S, n % SLOTS, :], bank[4 + n % 2][0:S, 0:T]).then_inc(t_copied, 1)

            with dve.Fori(0, G):
                go()
                layernorm(yn, yg, L0_EPS, 0)
                dve.wait_ge(v_zero, 1)
                for h in range(2):
                    dve.wait_ge(v_ps, h + 1)
                    for par in range(2):
                        halves = "p (s w d) -> p s w d"
                        V.tensor_copy(
                            vv[0:S, par, 2 * h:2 * h + 2, :].rearrange("p b n -> p (b n)").rearrange(halves, w=2, d=XD)[:, :, par, :],
                            bank[4 + h][0:S, :].rearrange(halves, w=2, d=XD)[:, :, par, :]).then_inc(v_ready, 1)
                attend(X, True)
                dve.wait_ge(bias_added, 1)
                for h in range(2):
                    dve.wait_ge(out_ps, h + 1)
                    last = V.tensor_tensor(x3[0:S, 2 * h:2 * h + 2, :], bank[h][0:S, :].rearrange("p (b d) -> p b d", b=2),
                                           x3[0:S, 2 * h:2 * h + 2, :], ALU.add)
                link(last)
                layernorm(yn, x3, L0_EPS, 1)
                for c in range(NODES):
                    for o in range(DC):
                        dve.wait_ge(e_ps, DC * c + o + 1)
                        V.tensor_scalar(node[c + 1][:, o, :], bank[6 + o][:, 0:T], ewc[:, c, 0:1], be_q[:, c, o:o + 1],
                                        ALU.mult, ALU.add).then_inc(e_ready, 1)
                    for h in range(2):
                        dve.wait_ge(v_ps, 2 * (c + 1) + h + 1)
                        V.tensor_scalar(vv[0:S, 0, 2 * h:2 * h + 2, :], bank[4 + h][0:S, :].rearrange("p (b d) -> p b d", b=2),
                                        ewc[0:S, c, 2:3], None, ALU.mult).then_inc(v_ready, 1)
                    attend(F[c], False)
                    for o in range(DC):
                        dve.wait_ge(out_ps, 2 + DC * c + o + 1)
                        V.scalar_tensor_tensor(node[c + 1][:, o, :], bank[o][:, 0:T], actw[:, c:c + 1], node[c + 1][:, o, :],
                                               ALU.mult, ALU.add).then_inc(node_ready, 1)
                for h in range(2):
                    dve.wait_ge(fin_ps, h + 1)
                    last = V.tensor_copy(yg[0:S, 2 * h:2 * h + 2, :], bank[2 + h][0:S, :].rearrange("p (b d) -> p b d", b=2))
                link(last)
                layernorm(yn, yg, DAG_EPS, 2)
                dve.wait_ge(norm_ready, 3 * NB)
                dve.wait_ge(bias_added, 2)
                link(V.tensor_tensor(yn[0:S], yn[0:S], ln_g[:].unsqueeze(1).to_broadcast([S, NB, D]), ALU.mult))
                V.tensor_tensor(x3[0:S], yn[0:S], x3[0:S], ALU.add).then_inc(result, 2)

        @block.gpsimd
        def _(pool):
            def go():
                pool.wait_ge(go_pool, 1)
                pool.sem_clear(go_pool)

            def rows_add(dst, src, bias, done):
                nc.gpsimd.tensor_tensor(dst[0:S], src[0:S], bias[:].unsqueeze(1).to_broadcast([S, NB, D]),
                                        ALU.add).then_inc(done, 1)

            with pool.Fori(0, G):
                go()
                rows_add(xb, xg, bias0, bias_added)

            with pool.Fori(0, G):
                go()
                nc.gpsimd.memset(vv[0:S], 0.0).then_inc(v_zero, 1)
                rows_add(x3, yg, bo1, bias_added)
                for n, *_ in X + [s for f in F for s in f]:
                    if n == len(X):
                        pool.wait_ge(norm_ready, 2 * NB)
                        rows_add(x3, x3, ln_b, bias_added)
                    pool.wait_ge(rinv_ready, n + 1)
                    if n >= 2:
                        pool.wait_ge(t_ps, n - 1)
                    nc.gpsimd.tensor_tensor(
                        pn[0:S, n % 2, :].rearrange("p (b s) -> p b s", b=NB),
                        pr[0:S, n % 2, :].rearrange("p (b s) -> p b s", b=NB),
                        rinv[:, n % RING, :].unsqueeze(2).to_broadcast([S, NB, S]), ALU.mult).then_inc(normed, 1)


def kernel(**inputs):
    from concourse import bacc
    from concourse.bass_utils import run_bass_kernel_spmd

    f = {k: np.asarray(v) for k, v in inputs.items()}

    def t(w):
        return np.swapaxes(w, -1, -2)

    def col(b):
        return t(b.reshape(*b.shape[:-1], DC, P))

    x = f["x"].reshape(B * S, D)
    ctx = f["ctx_1024"].reshape(B * SC, D)
    arrays = {"x": x, "ctx": ctx, "ctxT": t(ctx)}
    for name in ("L0_xattn_Wq", "L0_xattn_Wk", "L0_xattn_Wv", "L0_xattn_bo", "L0_ffn_gate_kernel", "L0_ffn_gate_bias",
                 "L0_ffn_w_gate", "L0_ffn_w_up", "L0_ffn_w_down", "L0_ffn_sw_gate", "L0_ffn_sw_up", "L0_ffn_sw_down",
                 "L1_xattn_bo", "L1_ffn_ew", "L1_ffn_act_w", "L1_ffn_We", "L1_ffn_Wq", "L1_ffn_Wk", "L1_ffn_Wv",
                 "L1_ffn_Wo", "L1_ffn_ln_g", "L1_ffn_ln_b"):
        arrays[name] = f[name]
    for name in ("L0_xattn_Wo", "L1_xattn_Wq", "L1_xattn_Wk", "L1_xattn_Wv", "L1_xattn_Wo", "L1_ffn_We"):
        arrays[name + "T"] = t(f[name])
    for name in ("L0_xattn_bq", "L0_xattn_bv", "L1_xattn_bq", "L1_xattn_bk", "L1_xattn_bv"):
        arrays[name] = col(f[name])
    arrays["L1_ffn_beT"] = col(f["L1_ffn_be"])
    i = np.arange(E)
    arrays["c_ident"] = np.eye(P, dtype=np.float32)
    arrays["c_causal"] = np.where(np.arange(S)[None, :] > np.arange(S)[:, None], MASKED, 0.0).astype(np.float32)
    arrays["c_half_mask"] = np.stack([(np.arange(P) // XD % 2 == par) for par in range(2)], 1).astype(np.float32)
    arrays["c_earlier"] = (i[None, :] < i[:, None]).astype(np.float32).reshape(-1)
    arrays["c_later_n"] = (E - 1 - i).astype(np.float32)
    arrays = {k: np.ascontiguousarray(v) for k, v in arrays.items()}

    nc = bacc.Bacc("TRN2", target_bir_lowering=False, num_devices=1)
    aps = {k: nc.dram_tensor(f"in_{k}", v.shape, mybir.dt.from_np(v.dtype), kind="ExternalInput").ap()
           for k, v in arrays.items()}
    out = nc.dram_tensor("out", (B * S, D), F32, kind="ExternalOutput").ap()
    build(nc, aps, out)
    r = run_bass_kernel_spmd(nc, [{f"in_{k}": v for k, v in arrays.items()}], core_ids=[0])
    return r.results[0]["out"].reshape(B, S, D)
```

```python
from contextlib import ExitStack

import concourse.bass as bass
import numpy as np
from concourse import mybir

ALU = mybir.AluOpType
ACT = mybir.ActivationFunctionType
AX = mybir.AxisListType.X
F32 = mybir.dt.float32
BF16 = mybir.dt.bfloat16
I32 = mybir.dt.int32

P = 128
B, S, D = 32, 112, 256
SC = 375
NT, CT = 3, 125
NB = 4
T = NB * S
G = B // NB
DC = D // P
E, M = 16, 128
NG, GE = 4, 4
XH, XD = 16, 16
NODES, PREV = 6, 5
FH, FD = 8, 32
STRIPS = 4
L0_EPS, DAG_EPS = 1e-5, 1e-6
MASKED = -1e30

DAG = []
_at = 0
for _c in range(NODES):
    _n = min(_c + 1, PREV)
    DAG.append(((_c - 1, _at + _n - 1), (_c - _n, _at), (_c - _n + _n // 2, _at + _n // 2)))
    _at += _n

HB = NB // 2
TH = HB * S
WINDOWS = 2 * (NODES + 1)
LAST = WINDOWS


def window_sets(w):
    batches = range(w % 2 * HB, w % 2 * HB + HB)
    return [(c, b, par) for c in range(DC) for b in batches for par in range(2 if w < 2 else 1)]


SETS, _n = [], 0
for _w in range(WINDOWS):
    SETS.append([(_n + i, *s) for i, s in enumerate(window_sets(_w))])
    _n += len(SETS[-1])


def lag(w):
    return 3 if w < 2 else 2


def steps(w):
    return len(SETS[w]) + lag(w)


def pieces(w):
    if w == 0:
        return {1: [("out", LAST)], 3: [("keys", 0)], 5: [("turn", 0)], 7: [("queries", 0)],
                8: [("values", 0), ("values_end", 0)], 9: [("final", LAST - 1)], 10: [("final", LAST)]}
    if w == 1:
        return {2: [("out", 1)], 5: [("turn", 1)], 6: [("edge", 1), ("keys", 1)], 7: [("queries", 1)],
                8: [("values", 1), ("values_end", 1)]}
    if w == 2:
        return {1: [("out", 2)], 4: [("turn", 2)],
                5: [(name, 2) for name in ("edge", "keys", "queries", "values", "values_end")]}
    if w < WINDOWS - 1:
        return {0: [("keys", w)], 2: [("out", w)], 3: [("edge", w)], 4: [("values", w), ("queries", w)],
                5: [("values_end", w)]}
    return {0: [("keys", -1)], 2: [("out", w)], 3: [("turn", -1), ("values", -1), ("values_end", -1)],
            4: [("queries", -1)]}


NORM_X3 = {1: ((1, 3), (1, 4), (1, 5)), 2: ((2, 2), (2, 3), (2, 4))}
NORM_FINAL = tuple((w, len(SETS[w]) + lag(w)) for w in (3, 4, 5))
NORM_NEXT = tuple((w, len(SETS[w]) + lag(w)) for w in (10, 11, 12))
NORMS = {1: 0, 2: HB, "final": 2 * HB, -1: 2 * HB + NB}

ORDER = [piece for w in range(WINDOWS) for i in range(steps(w)) for piece in pieces(w).get(i, [])]
BANK_ORDER = [piece for piece in ORDER if piece[0] != "values_end"]
NODE_OUTS = [r for name, r in ORDER if name == "out" and r > 2]


def rows(ap):
    return ap.rearrange("(c p) n -> p c n", p=P)


def build(nc, a, out):
    with ExitStack() as ctx:
        def sb(name, shape, dt=F32):
            return ctx.enter_context(nc.sbuf_tensor(name, shape, dt))

        def sem(name):
            return ctx.enter_context(nc.semaphore(name))

        bank = [ctx.enter_context(nc.psum_tensor(f"bank{i}", [P, 512], F32)) for i in range(8)]
        x2_dram = nc.dram_tensor("x2_scratch", [B * S, D], F32, kind="Internal").ap()

        x_wq, x_wk, x_wv, x_wo = (sb(f"x_w{n}", [P, DC, D]) for n in "qkvo")
        f_edge = sb("f_edge", [P, NODES, DC, D])
        f_wq = sb("f_wq", [P, NODES, DC, D])
        f_kk = sb("f_kk", [P, NODES, DC, D])
        f_vv = sb("f_vv", [P, NODES, DC, D])
        f_wo = sb("f_wo", [P, NODES, DC, D])

        ident = sb("ident", [P, P])
        causal = sb("causal", [S, S])
        earlier = sb("earlier", [S, E * E])
        later_n = sb("later_n", [S, E])
        gbias = sb("gbias", [S, E])
        bias0 = sb("bias0", [S, D])
        bo1 = sb("bo1", [S, D])
        ln_g = sb("ln_g", [S, D])
        ln_b = sb("ln_b", [S, D])
        half_mask = sb("half_mask", [P, 2])
        bq0 = sb("bq0", [P, DC])
        raw_bq0, raw_bv0 = sb("raw_bq0", [P, DC]), sb("raw_bv0", [P, DC])
        bq1, bk1, bv1 = sb("bq1", [P, DC]), sb("bk1", [P, DC]), sb("bv1", [P, DC])
        bq1_half = sb("bq1_half", [P, 2, DC])
        ewc = sb("ewc", [P, NODES, 3])
        actw = sb("actw", [P, NODES])
        be_in = sb("be_in", [P, 3, NODES, DC])
        be_q = sb("be_q", [P, NODES, DC])
        be_kv = sb("be_kv", [P, 2, NODES, DC])

        ARENA = 33800
        arena = sb("arena", [P, ARENA])
        at = [0]

        def cut(*shape):
            n = int(np.prod(shape))
            v = arena[:, at[0]:at[0] + n]
            at[0] += n
            assert at[0] <= ARENA, at[0]
            names = "abcd"[:len(shape)]
            if len(shape) == 1:
                return v
            return v.rearrange(f"p ({' '.join(names)}) -> p {' '.join(names)}", **dict(zip(names, shape)))

        score0 = cut(DC, D)
        value0 = cut(DC, D)
        gatek = cut(DC, E)
        w_gate = cut(E + 2, DC, M)
        w_up = cut(E + 2, DC, M)
        w_down = cut(E + 2, D)
        tiles_at = at[0]

        wk0, wq0, wv0, wo0 = cut(DC, D), cut(DC, D), cut(DC, D), cut(DC, D)
        weT = cut(2 * NODES, DC, D)
        wkv = cut(2 * NODES, DC, D)

        at[0] = tiles_at
        xg, xn, x1, xb = cut(NB, D), cut(NB, D), cut(NB, D), cut(NB, D)
        xnT = cut(DC, T)
        ctxg, ctxT = cut(NB, NT, D), cut(DC, NB * SC)
        shared_at = at[0]
        pr0 = cut(NB, SC)
        qT, oT = cut(DC, T), cut(DC, T)
        pT0 = cut(2, NT * S)
        at[0] = shared_at
        sig, choice = cut(NB, E), cut(NB, E)
        pmax, padd = cut(NB * NG, 2), cut(NB * NG, 2)
        gscore = cut(NB * NG)
        gless, glink = cut(NB, NG * NG), cut(NB, NG * NG)
        grank, gback = cut(NB, NG), cut(NB, NG)
        rank, back = cut(NB, E), cut(NB, E)
        comb, csum = cut(NB, E), cut(NB)
        less = cut(NB, E * E)
        combT = cut(T)
        th, inter = cut(2, T), cut(2, T)
        h1, h2 = cut(2, T), cut(2, T)

        at[0] = 0
        yg, x3 = cut(NB, D), cut(NB, D)
        cT = cut(DC, T)
        node = [cut(DC, T) for _ in range(NODES + 1)]
        keys = cut(DC, NB, STRIPS, S)
        qhT = cut(2, DC, T)
        aT = cut(DC, T)
        vx = cut(2, NB, D)
        vv = cut(NB, D)
        SLOTS = 3
        pr, pn = cut(SLOTS, STRIPS * S), cut(SLOTS, STRIPS * S)
        pT = cut(SLOTS, STRIPS * S)
        ynT = cut(DC, T)
        yn = cut(NB, D)
        res, yf = cut(NB, D), cut(NB, D)
        ident_h = cut(S // 2).bitcast(BF16)
        causal_h = cut(STRIPS * S // 2).bitcast(BF16)

        stats = sb("stats", [S, NB, 6])
        mv = sb("mv", [S, NB, 2])
        rs_v, rs_y, rs_t = sb("rs_v", [S, NB]), sb("rs_y", [S, NB]), sb("rs_t", [S, NB])
        RING = 8
        nmax, nbias = sb("nmax", [S, RING, NB]), sb("nbias", [S, RING, NB])
        rsum, rinv = sb("rsum", [S, RING, NB]), sb("rinv", [S, RING, NB])

        setup_loaded = sem("setup_loaded")
        fused = sem("fused")
        fused_copied = sem("fused_copied")
        loaded = sem("loaded")
        inputs_used = sem("inputs_used")
        vec = sem("vec")
        norm_ready = sem("norm_ready")
        turned = sem("turned")
        xnT_ready = sem("xnT_ready")
        q_ps, q_ready = sem("q_ps"), sem("q_ready")
        s_ps, max_ready = sem("s_ps"), sem("max_ready")
        exp_done = sem("exp_done")
        t_ps, t_copied = sem("t_ps"), sem("t_copied")
        o_ps, o_ready = sem("o_ps"), sem("o_ready")
        out_ps = sem("out_ps")
        bias_added = sem("bias_added")
        logit_ps, sig_ready = sem("logit_ps"), sem("sig_ready")
        comb_ready, combT_ps, combT_ready = sem("comb_ready"), sem("combT_ps"), sem("combT_ready")
        gu_ps, th_ready = sem("gu_ps"), sem("th_ready")
        h1_done, h2_done = sem("h1_done"), sem("h2_done")
        cb_ps, inter_ready, down_ps = sem("cb_ps"), sem("inter_ready"), sem("down_ps")
        k_ps, k_ready = sem("k_ps"), sem("k_ready")
        v_ps, v_ready = sem("v_ps"), sem("v_ready")
        e_ps, e_ready = sem("e_ps"), sem("e_ready")
        rinv_ready, normed = sem("rinv_ready"), sem("normed")
        x3_ready, node_ready = sem("x3_ready"), sem("node_ready")
        fin_ps, fin_ready = sem("fin_ps"), sem("fin_ready")
        scaled = sem("scaled")
        result = sem("result")
        stored = sem("stored")
        go_pe, go_act, go_dve, go_pool = sem("go_pe"), sem("go_act"), sem("go_dve"), sem("go_pool")
        counts = {}
        block = ctx.enter_context(nc.Block())

        PROJECTION_BANKS = (4, 5, 7)

        def projection_bank(name, r):
            return bank[PROJECTION_BANKS[BANK_ORDER.index((name, r)) % 3]]

        def nth(name, r, alone):
            return 1 if alone else [q for what, q in ORDER if what == name].index(r) + 1

        def nth_node(r, alone):
            return 1 if alone else NODE_OUTS.index(r) + 1

        @block.sync
        def _(sp):
            def release(*engines):
                sp.sem_clear(range(setup_loaded.num, stored.num + 1))
                for s in engines or (go_pe, go_act, go_dve, go_pool):
                    sp.sem_inc(s, 1)

            n = [0]

            def load(dst, src):
                n[0] += 16
                sp.dma_start(dst, src).then_inc(setup_loaded, 16)

            load(wq0[:], rows(a["L0_xattn_Wq"]))
            load(wk0[:], rows(a["L0_xattn_Wk"]))
            load(wv0[:], rows(a["L0_xattn_Wv"]))
            load(wo0[:], rows(a["L0_xattn_WoT"]))
            for i in range(NODES):
                load(weT[:, i], rows(a["L1_ffn_WeT"][DAG[i][1][1]]))
                load(weT[:, NODES + i], rows(a["L1_ffn_WeT"][DAG[i][2][1]]))
                load(f_edge[:, i], rows(a["L1_ffn_We"][DAG[i][0][1]]))
                load(wkv[:, i], rows(a["L1_ffn_Wk"][i]))
                load(wkv[:, NODES + i], rows(a["L1_ffn_Wv"][i]))
                load(f_wq[:, i], rows(a["L1_ffn_Wq"][i]))
                load(f_wo[:, i], rows(a["L1_ffn_Wo"][i]))
            load(x_wq[:], rows(a["L1_xattn_WqT"]))
            load(x_wk[:], rows(a["L1_xattn_WkT"]))
            load(x_wv[:], rows(a["L1_xattn_WvT"]))
            load(x_wo[:], rows(a["L1_xattn_WoT"]))
            load(gatek[:], rows(a["L0_ffn_gate_kernel"]))
            for c in range(DC):
                load(w_gate[:, 2:, c], a["L0_ffn_w_gate"][:, c * P:(c + 1) * P, :].rearrange("e p m -> p e m"))
                load(w_up[:, 2:, c], a["L0_ffn_w_up"][:, c * P:(c + 1) * P, :].rearrange("e p m -> p e m"))
                load(w_gate[:, 0:2, c], a["L0_ffn_sw_gate"][c * P:(c + 1) * P, :].rearrange("p (e m) -> p e m", m=M))
                load(w_up[:, 0:2, c], a["L0_ffn_sw_up"][c * P:(c + 1) * P, :].rearrange("p (e m) -> p e m", m=M))
            load(w_down[:, 2:], a["L0_ffn_w_down"].rearrange("e p n -> p e n"))
            load(w_down[:, 0:2], rows(a["L0_ffn_sw_down"]))
            load(ident[:], a["c_ident"])
            load(causal[:], a["c_causal"])
            load(half_mask[:], a["c_half_mask"])

            def to_all(dst, src):
                load(dst, src.partition_broadcast(dst.shape[0]))

            to_all(earlier[:], a["c_earlier"])
            to_all(later_n[:], a["c_later_n"])
            to_all(gbias[:], a["L0_ffn_gate_bias"])
            to_all(bias0[:], a["L0_xattn_bo"])
            to_all(bo1[:], a["L1_xattn_bo"])
            to_all(ln_g[:], a["L1_ffn_ln_g"])
            to_all(ln_b[:], a["L1_ffn_ln_b"])
            to_all(ewc[:].rearrange("p n k -> p (n k)"), a["L1_ffn_ew"].rearrange("n k -> (n k)"))
            to_all(actw[:], a["L1_ffn_act_w"])
            for dst, name in ((raw_bq0, "L0_xattn_bq"), (raw_bv0, "L0_xattn_bv"), (bq1, "L1_xattn_bq"),
                              (bk1, "L1_xattn_bk"), (bv1, "L1_xattn_bv")):
                load(dst[:], a[name])
            for i in range(NODES):
                for k in range(3):
                    load(be_in[:, k, i], a["L1_ffn_beT"][DAG[i][k][1]])
            sp.wait_ge(setup_loaded, n[0])
            counts["setup"] = n[0]

            def load_group(g):
                sp.dma_start(xg[0:S], a["x"][bass.ds(g * T, T), :].rearrange("(b s) d -> s b d", s=S)).then_inc(loaded, 16)
                for b in range(NB):
                    sp.dma_start(ctxg[0:CT, b], a["ctx"][bass.ds((g * NB + b) * SC, SC), :].rearrange(
                        "(t p) d -> p t d", p=CT)).then_inc(loaded, 16)
                sp.dma_start(ctxT[:], a["ctxT"][:, bass.ds(g * NB * SC, NB * SC)].rearrange(
                    "(c p) s -> p c s", p=P)).then_inc(loaded, 16)

            def store_group(g, dst, src):
                sp.wait_ge(result, 2)
                sp.dma_start(dst[bass.ds(g * T, T), :].rearrange("(b s) d -> s b d", s=S), src[0:S]).then_inc(stored, 16)
                sp.wait_ge(stored, 16)

            LOADS = 16 * (2 + NB)
            sp.wait_ge(result, 1)
            load_group(0)
            sp.wait_ge(loaded, LOADS)
            release()
            with sp.Fori(0, G - 1) as g:
                sp.wait_ge(inputs_used, 1)
                load_group(g + 1)
                store_group(g, x2_dram, xn)
                sp.wait_ge(loaded, LOADS)
                release()
            store_group(G - 1, x2_dram, xn)

            def load_group2(g):
                sp.dma_start(yg[0:S], x2_dram[bass.ds(g * T, T), :].rearrange("(b s) d -> s b d", s=S)).then_inc(loaded, 16)
                for c in range(DC):
                    sp.dma_start(cT[:, c].rearrange("p (b s) -> p b s", b=NB),
                                 a["ctxT"][c * P:(c + 1) * P, bass.ds(g * NB * SC, NB * SC)].rearrange(
                                     "p (b s) -> p b s", b=NB)[:, :, 0:S]).then_inc(loaded, 16)

            release(go_pool)
            sp.wait_ge(result, 1)
            LOADS2 = 16 * (1 + DC)
            load_group2(0)
            sp.wait_ge(loaded, LOADS2)
            release(go_pe, go_act, go_dve)
            for s in (k_ready, v_ready, q_ready):
                sp.wait_ge(s, 1)
            release()

            def store_group2(g):
                sp.wait_ge(result, 1)
                sp.dma_start(out[bass.ds(g * T, T), :].rearrange("(b s) d -> s b d", s=S), yf[0:S]).then_inc(stored, 16)
                sp.wait_ge(stored, 16)

            def group2(g, first, last):
                sp.wait_ge(inputs_used, 1)
                if last:
                    sp.sem_inc(loaded, LOADS2)
                else:
                    load_group2(g + 1)
                if first:
                    sp.wait_ge(result, 1)
                else:
                    store_group2(g - 1)
                for s, name in ((k_ready, "keys"), (v_ready, "values"), (q_ready, "queries")):
                    sp.wait_ge(s, nth(name, -1, False))
                sp.wait_ge(o_ready, WINDOWS)
                release()

            group2(0, True, False)
            with sp.Fori(1, G - 1) as g:
                group2(g, False, False)
            group2(G - 1, False, True)
            store_group2(G - 1)

        @block.tensor
        def _(pe):
            mm = nc.tensor.matmul

            pe.wait_ge(setup_loaded, counts["setup"])
            jobs = [(wq0, wk0), (wv0, wo0)] + [(weT[:, i], wkv[:, i]) for i in range(2 * NODES)]
            for i, (lhsT, rhs) in enumerate(jobs):
                if i >= 8:
                    pe.wait_ge(fused_copied, i - 7)
                for o in range(DC):
                    for c in range(DC):
                        last = mm(bank[i % 8][:, o * D:(o + 1) * D], lhsT[:, c, o * P:(o + 1) * P], rhs[:, c, :],
                                  start=(c == 0), stop=(c == DC - 1))
                last.then_inc(fused, 1)
            i = len(jobs)
            pe.wait_ge(fused_copied, i - 7)
            for o in range(DC):
                for c in range(DC):
                    mm(bank[i % 8][:, o:o + 1], wk0[:, c, o * P:(o + 1) * P], raw_bq0[:, c:c + 1],
                       start=(c == 0), stop=(c == DC - 1))
            for k in range(2 * NODES):
                for o in range(DC):
                    for c in range(DC):
                        last = mm(bank[i % 8][:, 2 + 2 * k + o:3 + 2 * k + o], wkv[:, k, c, o * P:(o + 1) * P],
                                  be_in[:, 1 + k // NODES, k % NODES, c:c + 1], start=(c == 0), stop=(c == DC - 1))
            last.then_inc(fused, 1)
            i += 1
            pe.wait_ge(fused_copied, i - 7)
            for c in range(DC):
                last = mm(bank[i % 8][0:S, 0:D], raw_bv0[:, c:c + 1].to_broadcast([P, S]), wo0[:, c, :],
                          start=(c == 0), stop=(c == DC - 1))
            last.then_inc(fused, 1)

            def go():
                pe.wait_ge(go_pe, 1)
                pe.sem_clear(go_pe)

            def turn(k):
                for b in range(NB):
                    pe.wait_ge(norm_ready, NB * k + b + 1)
                    for c in range(DC):
                        src = (xn if phase == 1 else yn)[0:S, b, c * P:(c + 1) * P]
                        last = nc.tensor.transpose(bank[c][:, b * S:(b + 1) * S], src, ident[0:S, 0:S])
                last.then_inc(turned, 1)

            def project(bank0, w, xT, done):
                for o in range(DC):
                    for c in range(DC):
                        last = mm(bank[bank0 + o][:, 0:T], w[:, c, o * P:(o + 1) * P], xT[:, c, :],
                                  start=(c == 0), stop=(c == DC - 1))
                    last.then_inc(done, 1)

            def project_tokens(bank0, xT, w, done):
                for b in range(NB):
                    for c in range(DC):
                        last = mm(bank[bank0 + b // 2][0:S, (b % 2) * D:(b % 2 + 1) * D],
                                  xT[:, c, b * S:(b + 1) * S], w[:, c, :], start=(c == 0), stop=(c == DC - 1))
                    if b % 2:
                        last.then_inc(done, 1)

            phase = 1
            with pe.Fori(0, G):
                go()
                turn(0)
                pe.wait_ge(xnT_ready, DC)
                project(2, score0, xnT, q_ps)
                pe.wait_ge(q_ready, DC)
                for b in range(NB):
                    for c in range(DC):
                        last = mm(bank[4 + b][0:S, 0:SC], qT[:, c, b * S:(b + 1) * S],
                                  ctxT[:, c, b * SC:(b + 1) * SC], start=(c == 0), stop=(c == DC - 1))
                    last.then_inc(s_ps, 1)
                for i in range(NB + 1):
                    if i < NB:
                        pe.wait_ge(exp_done, i + 1)
                        if i >= 2:
                            pe.wait_ge(t_copied, i - 1)
                        for t in range(NT):
                            last = nc.tensor.transpose(bank[i % 2][0:CT, t * S:(t + 1) * S],
                                                       pr0[0:S, i, t * CT:(t + 1) * CT], ident[0:S, 0:S])
                        last.then_inc(t_ps, 1)
                    if i >= 1:
                        b = i - 1
                        pe.wait_ge(t_copied, b + 1)
                        for c in range(DC):
                            for t in range(NT):
                                last = mm(bank[2 + c][:, b * S:(b + 1) * S], ctxg[0:CT, b, t, c * P:(c + 1) * P],
                                          pT0[0:CT, b % 2, t * S:(t + 1) * S], start=(t == 0), stop=(t == NT - 1))
                        last.then_inc(o_ps, 1)
                pe.wait_ge(o_ready, DC)
                project_tokens(0, oT, value0, out_ps)
                turn(1)
                pe.wait_ge(xnT_ready, 2 * DC)
                for b in range(NB):
                    for c in range(DC):
                        last = mm(bank[2][0:S, b * E:(b + 1) * E], xnT[:, c, b * S:(b + 1) * S], gatek[:, c, :],
                                  start=(c == 0), stop=(c == DC - 1))
                last.then_inc(logit_ps, 1)
                for k in range(E + 3):
                    if k < E + 2:
                        if k >= 4:
                            pe.wait_ge(h2_done, k - 3)
                        elif k >= 2:
                            pe.wait_ge(inter_ready, k - 1)
                        for w, bk in ((w_gate, 4), (w_up, 6)):
                            for c in range(DC):
                                last = mm(bank[bk + k % 2][:, 0:T], w[:, k, c, :], xnT[:, c, :],
                                          start=(c == 0), stop=(c == DC - 1))
                        last.then_inc(gu_ps, 1)
                    if k == 1:
                        pe.wait_ge(comb_ready, 1)
                        for b in range(NB):
                            last = nc.tensor.transpose(bank[3][0:E, b * S:(b + 1) * S], comb[0:S, b, :], ident[0:S, 0:S])
                        last.then_inc(combT_ps, 1)
                    if 2 <= k < E + 2:
                        pe.wait_ge(combT_ready, 1)
                        if k >= 4:
                            pe.wait_ge(inter_ready, k - 1)
                        mm(bank[2 + k % 2][:, 0:T], ident[0:E, k - 2:k - 1].to_broadcast([E, P]), combT[0:E, :],
                           start=True, stop=True).then_inc(cb_ps, 1)
                    if k >= 1:
                        pe.wait_ge(inter_ready, k)
                        for b in range(NB):
                            last = mm(bank[b // 2][0:S, (b % 2) * D:(b % 2 + 1) * D],
                                      inter[:, (k - 1) % 2, b * S:(b + 1) * S], w_down[:, k - 1, :],
                                      start=(k == 1 and b % 2 == 0), stop=(k == E + 2), skip_group_check=True)
                        last.then_inc(down_ps, 1)

            readouts = []

            def next_bank(name, r, s, n):
                if len(readouts) >= 3:
                    pe.wait_ge(*readouts[-3])
                readouts.append((s, n))
                return projection_bank(name, r)

            def project_half(bk, w, xT, h, done):
                for o in range(DC):
                    for i in range(DC):
                        last = mm(bk[:, o * TH:(o + 1) * TH], w[:, i, o * P:(o + 1) * P], xT[:, i, h * TH:(h + 1) * TH],
                                  start=(i == 0), stop=(i == DC - 1))
                last.then_inc(done, 1)

            def project_batch(bk, xT, w, h, b):
                for i in range(DC):
                    last = mm(bk[0:S, b * D:(b + 1) * D], xT[:, i, h * TH + b * S:h * TH + (b + 1) * S], w[:, i, :],
                              start=(i == 0), stop=(i == DC - 1))
                return last

            def piece(name, r, alone=False):
                h = 1 - r % 2
                c = (r - 1) // 2
                n = nth(name, r, alone)
                if name == "keys":
                    bk = next_bank(name, r, k_ready, n)
                    w, src = (x_wk, cT) if r <= 0 else (f_kk[:, c], node[DAG[c][1][0] + 1])
                    project_half(bk, w, src, h, k_ps)
                elif name in ("values", "values_end"):
                    b = 0
                    if name == "values":
                        bk = next_bank(name, r, v_ready, n)
                    else:
                        b, bk = 1, projection_bank("values", r)
                    w, src = (x_wv, cT) if r <= 0 else (f_vv[:, c], node[DAG[c][2][0] + 1])
                    last = project_batch(bk, src, w, h, b)
                    if b == 1:
                        last.then_inc(v_ps, 1)
                elif name == "turn":
                    bk = next_bank(name, r, xnT_ready, n)
                    for b in range(HB):
                        if r:
                            pe.wait_ge(norm_ready, (0 if alone else NORMS[r]) + b + 1)
                        for i in range(DC):
                            last = nc.tensor.transpose(bk[:, i * TH + b * S:i * TH + (b + 1) * S],
                                                       yn[0:S, h * HB + b, i * P:(i + 1) * P], ident[0:S, 0:S])
                    last.then_inc(turned, 1)
                elif name == "queries":
                    bk = next_bank(name, r, q_ready, n)
                    if r <= 0:
                        pe.wait_ge(xnT_ready, nth("turn", r, alone))
                        project_half(bk, x_wq, ynT, h, q_ps)
                    else:
                        pe.wait_ge(e_ready, nth("edge", r, alone))
                        project_half(bk, f_wq[:, c], node[c + 1], h, q_ps)
                elif name == "edge":
                    bk = next_bank(name, r, e_ready, n)
                    if r <= 2:
                        pe.wait_ge(xnT_ready, nth("turn", r, alone))
                    else:
                        pe.wait_ge(node_ready, nth_node(r, alone))
                    project_half(bk, f_edge[:, c], node[c], h, e_ps)
                elif name == "out":
                    if r < LAST:
                        pe.wait_ge(o_ready, r)
                    if r <= 2:
                        bk = next_bank(name, r, x3_ready, r)
                        for b in range(HB):
                            last = project_batch(bk, aT, x_wo, h, b)
                        last.then_inc(out_ps, 1)
                    else:
                        bk = next_bank(name, r, node_ready, nth_node(r, alone))
                        project_half(bk, f_wo[:, c - 1], aT, h, out_ps)
                elif name == "final":
                    bk = next_bank(name, r, fin_ready, r - LAST + 2)
                    if r == LAST:
                        pe.wait_ge(node_ready, 1)
                    for b in range(HB):
                        for i in range(DC):
                            last = nc.tensor.transpose(bk[0:S, b * D + i * P:b * D + (i + 1) * P],
                                                       node[NODES][:, i, h * TH + b * S:h * TH + (b + 1) * S], ident[:, :])
                    last.then_inc(fin_ps, 1)

            def scores(w, n, c, b, par):
                if n >= 3:
                    pe.wait_ge(exp_done, n - 2)
                last = mm(bank[n % 3][0:S, 0:T], qhT[:, par, c, b * S:(b + 1) * S],
                          keys[:, c, b].rearrange("p j s -> p (j s)"), start=True, stop=(w >= 2))
                if w < 2:
                    last = mm(bank[n % 3][0:S, 0:T], ident_h[0:S],
                              causal_h[0:S], start=False, stop=True)
                last.then_inc(s_ps, 1)

            def turn_probs(n):
                pe.wait_ge(normed, n + 1)
                if n:
                    pe.wait_ge(t_copied, n)
                for j in range(STRIPS):
                    last = nc.tensor.transpose(bank[3][0:S, j * S:(j + 1) * S],
                                               pn[0:S, n % SLOTS, j * S:(j + 1) * S], ident[0:S, 0:S])
                last.then_inc(t_ps, 1)

            def weigh(w, n, c, b, par):
                pe.wait_ge(t_copied, n + 1)
                for j in range(STRIPS):
                    col = c * P + 32 * j
                    last = mm(bank[6][32 * j:32 * j + 32, c * TH + b % HB * S:c * TH + (b % HB + 1) * S],
                              vx[0:S, par, b, col:col + 32] if w < 2 else vv[0:S, b, col:col + 32],
                              pT[0:S, n % SLOTS, j * S:(j + 1) * S], start=(par == 0), stop=(par == 1 or w >= 2))
                last.then_inc(o_ps, 1)

            go()
            for name in ("keys", "values", "values_end", "turn", "queries"):
                if name == "values":
                    pe.wait_ge(k_ready, 1)
                readouts.clear()
                piece(name, -1, alone=True)
            with pe.Fori(0, G):
                readouts.clear()
                go()
                for w in range(WINDOWS):
                    sets = SETS[w]
                    if w:
                        pe.wait_ge(k_ready, w)
                        pe.wait_ge(q_ready, w)
                    for i in range(steps(w)):
                        t, o = i - lag(w), i - lag(w) - 1
                        if i == 0 and w:
                            turn_probs(SETS[w - 1][-1][0])
                        if i < len(sets):
                            scores(w, *sets[i])
                        if o == 0 and w:
                            pe.wait_ge(v_ready, w)
                            pe.wait_ge(o_ready, w)
                        if o >= 0:
                            weigh(w, *sets[o])
                        if i == 1 and w:
                            weigh(w - 1, *SETS[w - 1][-1])
                        if 0 <= t < len(sets) - 1:
                            turn_probs(sets[t][0])
                        for name, r in pieces(w).get(i, []):
                            piece(name, r)
                turn_probs(SETS[-1][-1][0])
                weigh(WINDOWS - 1, *SETS[-1][-1])
            go()
            readouts.clear()
            piece("final", LAST - 1, alone=True)
            piece("out", LAST, alone=True)
            piece("final", LAST, alone=True)

        @block.scalar
        def _(act):
            def go():
                act.wait_ge(go_act, 1)
                act.sem_clear(go_act)

            def take_turned(k, dst):
                act.wait_ge(turned, k + 1)
                for c in range(DC):
                    nc.scalar.activation(dst[:, c, :], bank[c][:, 0:T], ACT.Identity).then_inc(xnT_ready, 1)

            with act.Fori(0, G):
                go()
                take_turned(0, xnT)
                for o in range(DC):
                    act.wait_ge(q_ps, o + 1)
                    nc.scalar.activation(qT[:, o, :], bank[2 + o][:, 0:T], ACT.Identity,
                                         bias=bq0[:, o:o + 1]).then_inc(q_ready, 1)
                for b in range(NB):
                    act.wait_ge(max_ready, b + 1)
                    nc.scalar.activation(pr0[0:S, b, :], bank[4 + b][0:S, 0:SC], ACT.Exp, bias=nbias[:, 0, b:b + 1],
                                         scale=float(D) ** -0.5, accum_out=rsum[:, 0, b:b + 1]).then_inc(exp_done, 1)
                act.wait_ge(o_ps, NB)
                for c in range(DC):
                    nc.scalar.activation(oT[:, c, :], bank[2 + c][:, 0:T], ACT.Identity).then_inc(o_ready, 1)
                take_turned(1, xnT)
                act.wait_ge(logit_ps, 1)
                nc.scalar.activation(sig[0:S], bank[2][0:S, 0:NB * E].rearrange("p (b e) -> p b e", b=NB),
                                     ACT.Tanh, scale=0.5).then_inc(sig_ready, 1)
                for k in range(E + 2):
                    act.wait_ge(gu_ps, k + 1)
                    if k >= 2:
                        act.wait_ge(h1_done, k - 1)
                    nc.scalar.activation(th[:, k % 2, :], bank[4 + k % 2][:, 0:T], ACT.Tanh,
                                         scale=0.5).then_inc(th_ready, 1)

            def take_keys(r, alone=False):
                h, c = 1 - r % 2, (r - 1) // 2
                bk = projection_bank("keys", r)
                act.wait_ge(k_ps, nth("keys", r, alone))
                for j, o in [(j, o) for j in range(STRIPS) for o in range(DC)]:
                    p = slice(32 * j, 32 * j + 32)
                    last = nc.scalar.activation(
                        keys[p, o, h * HB:(h + 1) * HB, j, :], bk[p, o * TH:(o + 1) * TH].rearrange("p (b s) -> p b s", b=HB),
                        ACT.Identity, bias=bk1[p, o:o + 1] if r <= 0 else be_kv[p, 0, c, o:o + 1],
                        scale=1.0 if r <= 0 else ewc[p, c, 1:2])
                last.then_inc(k_ready, 1)

            def take_values(r):
                h, c = 1 - r % 2, (r - 1) // 2
                act.wait_ge(v_ps, nth("values", r, False))
                nc.scalar.activation(vv[0:S, h * HB:(h + 1) * HB, :],
                                     projection_bank("values", r)[0:S, :].rearrange("p (b d) -> p b d", b=HB),
                                     ACT.Identity, scale=ewc[0:S, c, 2:3]).then_inc(v_ready, 1)

            def take_final(r):
                h = 1 - r % 2
                act.wait_ge(fin_ps, r - LAST + 2)
                nc.scalar.activation(yf[0:S, h * HB:(h + 1) * HB, :],
                                     projection_bank("final", r)[0:S, :].rearrange("p (b d) -> p b d", b=HB),
                                     ACT.Identity).then_inc(fin_ready, 1)

            def take_queries(r, alone=False):
                h = 1 - r % 2
                bk = projection_bank("queries", r)
                act.wait_ge(q_ps, nth("queries", r, alone))
                for o in range(DC):
                    for par in range(2):
                        last = nc.scalar.activation(qhT[:, par, o, h * TH:(h + 1) * TH], bk[:, o * TH:(o + 1) * TH],
                                                    ACT.Identity, scale=half_mask[:, par:par + 1],
                                                    bias=bq1_half[:, par, o:o + 1])
                last.then_inc(q_ready, 1)

            go()
            take_keys(-1, alone=True)
            take_queries(-1, alone=True)
            with act.Fori(0, G):
                go()
                for w in range(WINDOWS):
                    for i in range(steps(w) + 1):
                        if i < len(SETS[w]):
                            n = SETS[w][i][0]
                            act.wait_ge(max_ready, n + 1)
                            if n >= SLOTS:
                                act.wait_ge(normed, n - SLOTS + 1)
                            for j in range(STRIPS):
                                last = nc.scalar.activation(
                                    pr[0:S, n % SLOTS, j * S:(j + 1) * S], bank[n % 3][0:S, j * S:(j + 1) * S], ACT.Exp,
                                    bias=nbias[:, n % RING, j:j + 1], accum_out=rsum[:, n % RING, j:j + 1])
                            last.then_inc(exp_done, 1)
                        due = pieces(w).get(0, []) if i == 2 else []
                        due = due + (pieces(w).get(i - 1, []) if i >= 2 else [])
                        for name, r in due:
                            if name == "keys":
                                take_keys(r)
                            elif name == "values_end" and r > 0:
                                take_values(r)
                            elif name == "final":
                                take_final(r)
                            elif name == "queries" and r <= 0:
                                take_queries(r)
            go()
            take_final(LAST - 1)
            take_final(LAST)

        @block.vector
        def _(dve):
            V = nc.vector
            chain = [0]

            def link(ins):
                chain[0] += 1
                ins.then_inc(vec, 1)
                dve.wait_ge(vec, chain[0])

            def go():
                dve.wait_ge(go_dve, 1)
                dve.sem_clear(go_dve)
                chain[0] = normalized[0] = 0

            normalized = [0]

            def norm_stats(src):
                n = src.shape[1]
                if normalized[0]:
                    dve.wait_ge(norm_ready, normalized[0])
                for b in range(n):
                    last = V.bn_stats(stats[:, b, :], src[0:S, b, :])
                link(last)
                for b in range(n):
                    last = V.bn_aggr(mv[:, b, :], stats[:, b, :])
                link(last)

            def norm_rsqrt(eps, n):
                v, y, t = rs_v[:, 0:n], rs_y[:, 0:n], rs_t[:, 0:n]
                link(V.tensor_scalar(v, mv[:, 0:n, 1], eps, None, ALU.add))
                link(V.tensor_single_scalar(y.bitcast(I32), v.bitcast(I32), 1, ALU.arith_shift_right))
                link(V.tensor_scalar(y.bitcast(I32), y.bitcast(I32), -1.0, float(0x5F3759DF), ALU.mult, ALU.add))
                for _ in range(3):
                    link(V.tensor_tensor(t, v, y, ALU.mult))
                    link(V.scalar_tensor_tensor(t, t, -0.5, y, ALU.mult, ALU.mult))
                    link(V.scalar_tensor_tensor(y, t, 1.5, y, ALU.add, ALU.mult))

            def norm_apply(dst, src):
                for b in range(src.shape[1]):
                    V.tensor_scalar(dst[0:S, b, :], src[0:S, b, :], mv[:, b, 0:1], rs_y[:, b:b + 1],
                                    ALU.subtract, ALU.mult).then_inc(norm_ready, 1)
                normalized[0] += src.shape[1]

            def layernorm(dst, src, eps):
                norm_stats(src)
                norm_rsqrt(eps, src.shape[1])
                norm_apply(dst, src)

            dve.wait_ge(setup_loaded, counts["setup"])
            link(V.tensor_scalar(half_mask[:], half_mask[:], float(XD) ** -0.5, None, ALU.mult))
            for par in range(2):
                V.tensor_scalar(bq1_half[:, par, :], bq1[:], half_mask[:, par:par + 1], None, ALU.mult)
            V.tensor_tensor(be_q[:], be_in[:, 0], ewc[:, :, 0:1].to_broadcast([P, NODES, DC]), ALU.mult)
            dsts = [score0[:], value0[:]] + [f_kk[:, i] for i in range(NODES)] + [f_vv[:, i] for i in range(NODES)]
            for i, dst in enumerate(dsts):
                dve.wait_ge(fused, i + 1)
                V.tensor_copy(dst, bank[i % 8][:, :].rearrange("p (c n) -> p c n", c=DC)).then_inc(fused_copied, 1)
            i = len(dsts)
            dve.wait_ge(fused, i + 1)
            V.tensor_copy(bq0[:], bank[i % 8][:, 0:DC])
            for k in range(2):
                last = V.tensor_tensor(be_kv[:, k], bank[i % 8][:, 2 + k * NODES * DC:2 + (k + 1) * NODES * DC].rearrange(
                    "p (n c) -> p n c", c=DC), ewc[:, :, 1 + k:2 + k].to_broadcast([P, NODES, DC]), ALU.mult)
            last.then_inc(fused_copied, 1)
            dve.wait_ge(fused, i + 2)
            V.tensor_tensor(bias0[:], bank[(i + 1) % 8][0:S, 0:D], bias0[:], ALU.add).then_inc(result, 1)

            def route():
                s64 = choice[0:S]
                link(V.tensor_scalar(s64, sig[0:S], 0.5, 0.5, ALU.mult, ALU.add))
                link(V.tensor_tensor(s64, s64, gbias[:].unsqueeze(1).to_broadcast([S, NB, E]), ALU.add))
                quads = s64.rearrange("p b (g h w) -> p (b g) h w", g=NG, h=2)
                V.tensor_tensor(pmax[0:S], quads[:, :, :, 0], quads[:, :, :, 1], ALU.max)
                link(V.tensor_tensor(padd[0:S], quads[:, :, :, 0], quads[:, :, :, 1], ALU.add))
                link(V.tensor_tensor(gscore[0:S], pmax[0:S, :, 0], pmax[0:S, :, 1], ALU.add))
                for h in range(2):
                    link(V.tensor_tensor(gscore[0:S], gscore[0:S], padd[0:S, :, h], ALU.max))

                def ranks(v, n, less_, rank_, back_):
                    sq = [S, NB, n, n]
                    L = less_[0:S].rearrange("p b (i j) -> p b i j", i=n)
                    for b in range(NB):
                        last_ = V.tensor_tensor(L[:, b], v[:, b, :].unsqueeze(1).to_broadcast([S, n, n]),
                                                v[:, b, :].unsqueeze(2).to_broadcast([S, n, n]), ALU.is_ge)
                    link(last_)
                    e_ = earlier[:].rearrange("p (i j) -> p i j", i=E)[:, 0:n, 0:n]
                    for b in range(NB):
                        last_ = V.tensor_tensor(L[:, b], L[:, b], e_, ALU.mult)
                    link(last_)
                    V.tensor_reduce(rank_[0:S], L, axis=AX, op=ALU.add)
                    link(V.tensor_reduce(back_[0:S], L.rearrange("p b i j -> p b j i"), axis=AX, op=ALU.add))
                    link(V.tensor_tensor(rank_[0:S], rank_[0:S], back_[0:S], ALU.subtract))
                    link(V.tensor_tensor(rank_[0:S], rank_[0:S],
                                         later_n[:, E - n:E].unsqueeze(1).to_broadcast([S, NB, n]), ALU.add))

                ranks(gscore[0:S].rearrange("p (b g) -> p b g", b=NB), NG, gless, grank, gback)
                link(V.tensor_single_scalar(grank[0:S], grank[0:S], 1.5, ALU.is_lt))
                link(V.tensor_tensor(s64.rearrange("p b (g w) -> p (b g) w", g=NG), s64.rearrange("p b (g w) -> p (b g) w", g=NG),
                                     grank[0:S].rearrange("p b g -> p (b g)").unsqueeze(2).to_broadcast([S, NB * NG, GE]), ALU.mult))
                ranks(s64, E, less, rank, back)
                link(V.scalar_tensor_tensor(comb[0:S], rank[0:S], 3.5, s64, ALU.is_lt, ALU.mult))
                link(V.tensor_reduce(csum[0:S], comb[0:S], axis=AX, op=ALU.add))
                link(V.tensor_scalar(csum[0:S], csum[0:S], 1e-20, None, ALU.add))
                link(V.reciprocal(csum[0:S], csum[0:S]))
                V.scalar_tensor_tensor(comb[0:S], comb[0:S], 2.5, csum[0:S].unsqueeze(2).to_broadcast([S, NB, E]),
                                       ALU.mult, ALU.mult).then_inc(comb_ready, 1)

            with dve.Fori(0, G):
                go()
                layernorm(xn, xg, L0_EPS)
                for b in range(NB):
                    dve.wait_ge(s_ps, b + 1)
                    link(V.tensor_reduce(nmax[:, 0, b:b + 1], bank[4 + b][0:S, 0:SC], axis=AX, op=ALU.max))
                    V.tensor_scalar(nbias[:, 0, b:b + 1], nmax[:, 0, b:b + 1], -float(D) ** -0.5, None,
                                    ALU.mult).then_inc(max_ready, 1)
                for b in range(NB):
                    dve.wait_ge(t_ps, b + 1)
                    if b >= 2:
                        dve.wait_ge(o_ps, b - 1)
                    V.tensor_copy(pT0[0:CT, b % 2, :], bank[b % 2][0:CT, 0:NT * S]).then_inc(t_copied, 1)
                dve.wait_ge(exp_done, NB)
                link(V.reciprocal(rinv[:, 0, :], rsum[:, 0, :]))
                dve.wait_ge(bias_added, 1)
                for b in range(NB):
                    dve.wait_ge(out_ps, b // 2 + 1)
                    last = V.scalar_tensor_tensor(x1[0:S, b, :], bank[b // 2][0:S, (b % 2) * D:(b % 2 + 1) * D],
                                                  rinv[:, 0, b:b + 1], xb[0:S, b, :], ALU.mult, ALU.add)
                last.then_inc(inputs_used, 1)
                dve.wait_ge(inputs_used, 1)
                layernorm(xn, x1, L0_EPS)
                dve.wait_ge(sig_ready, 1)
                route()
                for k in range(E + 2):
                    dve.wait_ge(th_ready, k + 1)
                    if k >= 2:
                        dve.wait_ge(inter_ready, k - 1)
                    V.scalar_tensor_tensor(h1[:, k % 2, :], th[:, k % 2, :], 1.0, bank[4 + k % 2][:, 0:T],
                                           ALU.add, ALU.mult).then_inc(h1_done, 1)
                    dve.wait_ge(h1_done, k + 1)
                    if k >= 2:
                        dve.wait_ge(down_ps, k - 1)
                    if k < 2:
                        V.scalar_tensor_tensor(inter[:, k % 2, :], h1[:, k % 2, :], 0.5, bank[6 + k % 2][:, 0:T],
                                               ALU.mult, ALU.mult).then_inc(inter_ready, 1)
                    else:
                        V.scalar_tensor_tensor(h2[:, k % 2, :], h1[:, k % 2, :], 0.5, bank[6 + k % 2][:, 0:T],
                                               ALU.mult, ALU.mult).then_inc(h2_done, 1)
                        dve.wait_ge(h2_done, k - 1)
                        dve.wait_ge(cb_ps, k - 1)
                        V.tensor_tensor(inter[:, k % 2, :], h2[:, k % 2, :], bank[2 + k % 2][:, 0:T], ALU.mult).then_inc(inter_ready, 1)
                    if k == 0:
                        dve.wait_ge(combT_ps, 1)
                        V.tensor_copy(combT[0:E, :], bank[3][0:E, 0:T]).then_inc(combT_ready, 1)
                dve.wait_ge(down_ps, E + 2)
                for h in range(2):
                    V.tensor_tensor(xn[0:S, 2 * h:2 * h + 2, :], bank[h][0:S, :].rearrange("p (b d) -> p b d", b=2),
                                    x1[0:S, 2 * h:2 * h + 2, :], ALU.add).then_inc(result, 1)

            def evacuate(name, r, alone=False):
                h = 1 - r % 2
                c = (r - 1) // 2
                bk = projection_bank("values" if name == "values_end" else name, r)
                batches, cols = slice(h * HB, (h + 1) * HB), slice(h * TH, (h + 1) * TH)
                by_batch = bk[0:S, :].rearrange("p (b d) -> p b d", b=HB)
                by_chunk = bk[:, 0:T].rearrange("p (c s) -> p c s", c=DC)
                if name == "values_end" and r <= 0:
                    dve.wait_ge(v_ps, nth(name, r, alone))
                    for par in range(2):
                        halves = "p (s w d) -> p s w d"
                        last = V.tensor_copy(
                            vx[0:S, par, batches, :].rearrange("p b n -> p (b n)").rearrange(halves, w=2, d=XD)[:, :, par, :],
                            bk[0:S, :].rearrange(halves, w=2, d=XD)[:, :, par, :])
                    last.then_inc(v_ready, 1)
                elif name == "turn":
                    dve.wait_ge(turned, nth(name, r, alone))
                    V.tensor_copy((ynT if r <= 0 else node[0])[:, :, cols], by_chunk).then_inc(xnT_ready, 1)
                elif name == "queries" and r >= 1:
                    dve.wait_ge(q_ps, nth(name, r, alone))
                    V.tensor_scalar(qhT[:, 0, :, cols], by_chunk, float(FD) ** -0.5, None, ALU.mult).then_inc(q_ready, 1)
                elif name == "edge":
                    dve.wait_ge(e_ps, r)
                    for o in range(DC):
                        last = V.tensor_scalar(node[c + 1][:, o, cols], by_chunk[:, o, :], ewc[:, c, 0:1],
                                               be_q[:, c, o:o + 1], ALU.mult, ALU.add)
                    last.then_inc(e_ready, 1)
                elif name == "out":
                    dve.wait_ge(out_ps, nth(name, r, alone))
                    if r <= 2:
                        dve.wait_ge(bias_added, 1)
                        V.tensor_tensor(x3[0:S, batches, :], by_batch, x3[0:S, batches, :], ALU.add).then_inc(x3_ready, 1)
                    else:
                        for o in range(DC):
                            last = V.scalar_tensor_tensor(node[c][:, o, cols], by_chunk[:, o, :], actw[:, c - 1:c],
                                                          node[c][:, o, cols], ALU.mult, ALU.add)
                        last.then_inc(node_ready, 1)

            def take_output(r):
                h, c = 1 - r % 2, (r - 1) // 2
                dve.wait_ge(o_ps, SETS[r - 1][-1][0] + 1)
                for o in range(DC):
                    bias = bv1[:, o:o + 1] if r <= 2 else be_kv[:, 1, c - 1, o:o + 1]
                    last = V.tensor_scalar(aT[:, o, h * TH:(h + 1) * TH], bank[6][:, o * TH:(o + 1) * TH], bias, None,
                                           ALU.add)
                last.then_inc(o_ready, 1)

            def copy_probs(n):
                dve.wait_ge(t_ps, n + 1)
                if n >= SLOTS:
                    dve.wait_ge(o_ps, n - SLOTS + 1)
                V.tensor_copy(pT[0:S, n % SLOTS, :], bank[3][0:S, 0:T]).then_inc(t_copied, 1)

            def invert_sums(n):
                dve.wait_ge(exp_done, n + 1)
                if n >= RING:
                    dve.wait_ge(normed, n - RING + 1)
                V.reciprocal(rinv[:, n % RING, :], rsum[:, n % RING, :]).then_inc(rinv_ready, 1)

            def norm_step(at):
                for r, when in NORM_X3.items():
                    batches = slice((r - 1) * HB, r * HB)
                    if at == when[0]:
                        dve.wait_ge(x3_ready, r)
                        norm_stats(x3[:, batches])
                    if at == when[1]:
                        norm_rsqrt(L0_EPS, HB)
                    if at == when[2]:
                        norm_apply(yn[:, batches], x3[:, batches])
                if at == NORM_FINAL[0]:
                    dve.wait_ge(fin_ready, 2)
                    norm_stats(yf)
                if at == NORM_FINAL[1]:
                    norm_rsqrt(DAG_EPS, NB)
                if at == NORM_FINAL[2]:
                    norm_apply(yf, yf)
                if at == NORM_NEXT[0]:
                    dve.wait_ge(loaded, 16 * (1 + DC))
                    norm_stats(yg)
                if at == NORM_NEXT[1]:
                    norm_rsqrt(L0_EPS, NB)
                if at == NORM_NEXT[2]:
                    norm_apply(yn, yg)

            go()
            layernorm(yn, yg, L0_EPS)
            for name in ("values_end", "turn"):
                evacuate(name, -1, alone=True)
            with dve.Fori(0, G):
                go()
                for w in range(WINDOWS):
                    for i in range(steps(w) + 1):
                        t = i - lag(w)
                        if i == 0 and w:
                            copy_probs(SETS[w - 1][-1][0])
                        due = pieces(w).get(0, []) if i == 2 else []
                        due = due + (pieces(w).get(i - 1, []) if i >= 2 else [])
                        for name, r in due:
                            evacuate(name, r)
                        if i < steps(w):
                            norm_step((w, i))
                        if i == 1 and w >= 2:
                            invert_sums(SETS[w][0][0])
                        if i < len(SETS[w]):
                            n = SETS[w][i][0]
                            dve.wait_ge(s_ps, n + 1)
                            V.tensor_reduce(nbias[:, n % RING, :], bank[n % 3][0:S, 0:T].rearrange(
                                "p (j s) -> p j s", j=STRIPS), axis=AX, op=ALU.max, negate=True).then_inc(max_ready, 1)
                        if (1 if w < 2 else 2) <= i <= len(SETS[w]):
                            invert_sums(SETS[w][i - 1][0])
                        if i == 1 and w:
                            take_output(w)
                        if 0 <= t < len(SETS[w]) - 1:
                            copy_probs(SETS[w][t][0])
                        if (w, i) == (2, 5):
                            V.tensor_copy(rs_t[:, 0:1], rs_y[:, 0:1]).then_inc(inputs_used, 1)
                        if i == steps(w):
                            norm_step((w, i))
                copy_probs(SETS[-1][-1][0])
                take_output(LAST)
            go()
            evacuate("out", LAST, alone=True)
            dve.wait_ge(fin_ready, 2)
            layernorm(yf, yf, DAG_EPS)

        @block.gpsimd
        def _(pool):
            def go():
                pool.wait_ge(go_pool, 1)
                pool.sem_clear(go_pool)

            def rows_add(dst, src, bias, done):
                nc.gpsimd.tensor_tensor(dst[0:S], src[0:S], bias[:].unsqueeze(1).to_broadcast([S, NB, D]),
                                        ALU.add).then_inc(done, 1)

            with pool.Fori(0, G):
                go()
                rows_add(xb, xg, bias0, bias_added)

            go()
            nc.gpsimd.memset(keys[:], 0.0)
            nc.gpsimd.memset(vx[0:S], 0.0)
            nc.gpsimd.tensor_copy(ident_h[0:S], ident[0:S, 0:S])
            nc.gpsimd.tensor_copy(causal_h[0:S].rearrange("p (j s) -> p j s", j=STRIPS),
                                  causal[:].unsqueeze(1).to_broadcast([S, STRIPS, S]))
            for tile in (aT, node[NODES], res):
                last = nc.gpsimd.memset(tile[:], 0.0)
            last.then_inc(result, 1)

            def finish(normalized):
                pool.wait_ge(norm_ready, normalized)
                nc.gpsimd.tensor_tensor(yf[0:S], yf[0:S], ln_g[:].unsqueeze(1).to_broadcast([S, NB, D]),
                                        ALU.mult).then_inc(scaled, 1)
                pool.wait_ge(scaled, 1)
                nc.gpsimd.tensor_tensor(yf[0:S], yf[0:S], res[0:S], ALU.add).then_inc(result, 1)

            with pool.Fori(0, G):
                go()
                rows_add(x3, yg, bo1, bias_added)
                for w in range(WINDOWS):
                    for n, *_ in SETS[w]:
                        pool.wait_ge(rinv_ready, n + 1)
                        if n >= SLOTS:
                            pool.wait_ge(t_ps, n - SLOTS + 1)
                        nc.gpsimd.tensor_tensor(
                            pn[0:S, n % SLOTS, :].rearrange("p (j s) -> p j s", j=STRIPS),
                            pr[0:S, n % SLOTS, :].rearrange("p (j s) -> p j s", j=STRIPS),
                            rinv[:, n % RING, :].unsqueeze(2).to_broadcast([S, STRIPS, S]), ALU.mult).then_inc(normed, 1)
                    if w == NORM_FINAL[-1][0]:
                        finish(NORMS["final"] + NB)
                    if w == 8:
                        pool.wait_ge(x3_ready, 2)
                        pool.wait_ge(result, 1)
                        rows_add(res, x3, ln_b, bias_added)
            go()
            finish(NB)


def kernel(**inputs):
    from concourse import bacc
    from concourse.bass_utils import run_bass_kernel_spmd

    f = {k: np.asarray(v) for k, v in inputs.items()}

    def t(w):
        return np.swapaxes(w, -1, -2)

    def col(b):
        return t(b.reshape(*b.shape[:-1], DC, P))

    x = f["x"].reshape(B * S, D)
    ctx = f["ctx_1024"].reshape(B * SC, D)
    arrays = {"x": x, "ctx": ctx, "ctxT": t(ctx)}
    for name in ("L0_xattn_Wq", "L0_xattn_Wk", "L0_xattn_Wv", "L0_xattn_bo", "L0_ffn_gate_kernel", "L0_ffn_gate_bias",
                 "L0_ffn_w_gate", "L0_ffn_w_up", "L0_ffn_w_down", "L0_ffn_sw_gate", "L0_ffn_sw_up", "L0_ffn_sw_down",
                 "L1_xattn_bo", "L1_ffn_ew", "L1_ffn_act_w", "L1_ffn_We", "L1_ffn_Wq", "L1_ffn_Wk", "L1_ffn_Wv",
                 "L1_ffn_Wo", "L1_ffn_ln_g", "L1_ffn_ln_b"):
        arrays[name] = f[name]
    for name in ("L0_xattn_Wo", "L1_xattn_Wq", "L1_xattn_Wk", "L1_xattn_Wv", "L1_xattn_Wo", "L1_ffn_We"):
        arrays[name + "T"] = t(f[name])
    for name in ("L0_xattn_bq", "L0_xattn_bv", "L1_xattn_bq", "L1_xattn_bk", "L1_xattn_bv"):
        arrays[name] = col(f[name])
    arrays["L1_ffn_beT"] = col(f["L1_ffn_be"])
    i = np.arange(E)
    arrays["c_ident"] = np.eye(P, dtype=np.float32)
    arrays["c_causal"] = np.where(np.arange(S)[None, :] > np.arange(S)[:, None], MASKED, 0.0).astype(np.float32)
    arrays["c_half_mask"] = np.stack([(np.arange(P) // XD % 2 == par) for par in range(2)], 1).astype(np.float32)
    arrays["c_earlier"] = (i[None, :] < i[:, None]).astype(np.float32).reshape(-1)
    arrays["c_later_n"] = (E - 1 - i).astype(np.float32)
    arrays = {k: np.ascontiguousarray(v) for k, v in arrays.items()}

    nc = bacc.Bacc("TRN2", target_bir_lowering=False, num_devices=1)
    aps = {k: nc.dram_tensor(f"in_{k}", v.shape, mybir.dt.from_np(v.dtype), kind="ExternalInput").ap()
           for k, v in arrays.items()}
    out = nc.dram_tensor("out", (B * S, D), F32, kind="ExternalOutput").ap()
    build(nc, aps, out)
    r = run_bass_kernel_spmd(nc, [{f"in_{k}": v for k, v in arrays.items()}], core_ids=[0])
    return r.results[0]["out"].reshape(B, S, D)
```

```python
from contextlib import ExitStack

import concourse.bass as bass
import numpy as np
from concourse import mybir

ALU = mybir.AluOpType
ACT = mybir.ActivationFunctionType
AX = mybir.AxisListType.X
F32 = mybir.dt.float32
F32R = mybir.dt.float32r
BF16 = mybir.dt.bfloat16
I32 = mybir.dt.int32

P = 128
B, S, D = 32, 112, 256
SC = 375
NT, CT = 3, 125
NB = 4
T = NB * S
G = B // NB
DC = D // P
E, M = 16, 128
NG, GE = 4, 4
XD = 16
NODES, PREV = 6, 5
FD = 32
STRIPS = 4
L0_EPS, DAG_EPS = 1e-5, 1e-6
MASKED = -1e30

DAG = []
_at = 0
for _c in range(NODES):
    _n = min(_c + 1, PREV)
    DAG.append(((_c - 1, _at + _n - 1), (_c - _n, _at), (_c - _n + _n // 2, _at + _n // 2)))
    _at += _n

HB = NB // 2
TH = HB * S
WINDOWS = 2 * (NODES + 1)
LAST = WINDOWS


def window_sets(w):
    batches = range(w % 2 * HB, w % 2 * HB + HB)
    return [(c, b, par) for c in range(DC) for b in batches for par in range(2 if w < 2 else 1)]


SETS, _n = [], 0
for _w in range(WINDOWS):
    SETS.append([(_n + i, *s) for i, s in enumerate(window_sets(_w))])
    _n += len(SETS[-1])


def lag(w):
    return 3 if w < 2 else 2


def steps(w):
    return len(SETS[w]) + lag(w)


def pieces(w):
    if w == 0:
        return {1: [("out", LAST)], 3: [("keys", 0)], 5: [("turn", 0)], 7: [("queries", 0)],
                8: [("values", 0), ("values_end", 0)], 9: [("final", LAST - 1)], 10: [("final", LAST)]}
    if w == 1:
        return {2: [("out", 1)], 7: [("turn", 1)], 8: [("edge", 1), ("keys", 1)], 9: [("queries", 1)],
                10: [("values", 1), ("values_end", 1)]}
    if w == 2:
        return {1: [("out", 2)], 4: [("turn", 2)],
                5: [(name, 2) for name in ("edge", "keys", "queries", "values", "values_end")]}
    if w < WINDOWS - 1:
        return {0: [("keys", w)], 2: [("out", w)], 3: [("edge", w)], 4: [("values", w), ("queries", w)],
                5: [("values_end", w)]}
    return {0: [("keys", -1)], 2: [("out", w)], 3: [("turn", -1)], 4: [("queries", -1)],
            5: [("values", -1), ("values_end", -1)]}


NORM_X3 = {1: ((1, 3), (1, 4), (1, 5), (1, 6), (1, 7)), 2: ((2, 2), (2, 3), (2, 3), (2, 4), (2, 4))}
NORM_FROM, NORM_STEPS = 3, 9
FINAL_DONE = NORM_FROM + (NORM_STEPS - 1) // 2
NORMS = {1: 0, 2: HB, "final": 2 * HB, -1: 2 * HB + NB}

SHARED_KEYS = (1, 2)

ORDER = [piece for w in range(WINDOWS) for i in range(steps(w)) for piece in pieces(w).get(i, [])]
BANK_ORDER = [piece for piece in ORDER if piece[0] != "values_end"]
NODE_OUTS = [r for name, r in ORDER if name == "out" and r > 2]


def rows(ap):
    return ap.rearrange("(c p) n -> p c n", p=P)


def build(nc, a, out):
    with ExitStack() as ctx:
        def sb(name, shape, dt=F32):
            return ctx.enter_context(nc.sbuf_tensor(name, shape, dt))

        def sem(name):
            return ctx.enter_context(nc.semaphore(name))

        bank = [ctx.enter_context(nc.psum_tensor(f"bank{i}", [P, 512], F32)) for i in range(8)]
        x2_dram = nc.dram_tensor("x2_scratch", [B * S, D], F32, kind="Internal").ap()

        x_wq, x_wk, x_wv, x_wo = (sb(f"x_w{n}", [P, DC, D]) for n in "qkvo")
        f_kk = sb("f_kk", [P, NODES, DC, D])
        f_vv = sb("f_vv", [P, NODES, DC, D])

        with ExitStack() as phase1_only:
            def sb_r(name, shape):
                return phase1_only.enter_context(nc.sbuf_tensor(name, shape, F32R))

            w_gu = sb_r("w_gu", [P, 2, 2, DC, 2, M])
            w_dn = sb_r("w_dn", [P, 2, 2, D])
            xr = sb_r("xr", [P, DC, 2, T])
            inr = sb_r("inr", [P, 2, 2, T])
            combr = sb_r("combr", [E, 2, T])
            ident_e = sb_r("ident_e", [E, E])
        f_edge = sb("f_edge", [P, NODES, DC, D])
        f_wq = sb("f_wq", [P, NODES, DC, D])
        f_wo = sb("f_wo", [P, NODES, DC, D])

        ident = sb("ident", [P, P])
        causal = sb("causal", [S, S])
        earlier = sb("earlier", [S, E * E])
        later_n = sb("later_n", [S, E])
        gbias = sb("gbias", [S, E])
        bias0 = sb("bias0", [S, D])
        bo1 = sb("bo1", [S, D])
        ln_g = sb("ln_g", [S, D])
        ln_b = sb("ln_b", [S, D])
        half_mask = sb("half_mask", [P, 2])
        bq0 = sb("bq0", [P, DC])
        raw_bq0, raw_bv0 = sb("raw_bq0", [P, DC]), sb("raw_bv0", [P, DC])
        bq1, bk1, bv1 = sb("bq1", [P, DC]), sb("bk1", [P, DC]), sb("bv1", [P, DC])
        bq1_half = sb("bq1_half", [P, 2, DC])
        ewc = sb("ewc", [P, NODES, 3])
        actw = sb("actw", [P, NODES])
        be_in = sb("be_in", [P, 3, NODES, DC])
        be_q = sb("be_q", [P, NODES, DC])
        be_kv = sb("be_kv", [P, 2, NODES, DC])

        ARENA = 33800
        arena = sb("arena", [P, ARENA])
        at = [0]

        def cut(*shape):
            n = int(np.prod(shape))
            v = arena[:, at[0]:at[0] + n]
            at[0] += n
            assert at[0] <= ARENA, at[0]
            names = "abcd"[:len(shape)]
            if len(shape) == 1:
                return v
            return v.rearrange(f"p ({' '.join(names)}) -> p {' '.join(names)}", **dict(zip(names, shape)))

        score0 = cut(DC, D)
        value0 = cut(DC, D)
        gatek = cut(DC, E)
        w_gate = cut(E + 2, DC, M)
        w_up = cut(E + 2, DC, M)
        w_down = cut(E + 2, D)
        tiles_at = at[0]

        ARENA_PHASE0 = 28 * DC * D
        at[0] = ARENA - ARENA_PHASE0
        wk0, wq0, wv0, wo0 = cut(DC, D), cut(DC, D), cut(DC, D), cut(DC, D)
        weT = cut(2 * NODES, DC, D)
        wkv = cut(2 * NODES, DC, D)

        at[0] = tiles_at
        xg, xnext = cut(NB, D), cut(NB, D)
        assert at[0] <= ARENA - ARENA_PHASE0
        xn, x1, xb = cut(NB, D), cut(NB, D), cut(NB, D)
        xnT, qT = cut(DC, T), cut(DC, T)
        ctxg, ctxT = cut(NB, NT, D), cut(DC, NB * SC)
        shared_at = at[0]
        pr0 = cut(NB, SC)
        oT = cut(DC, T)
        pT0 = cut(2, NT * S)
        at[0] = shared_at
        sig, choice = cut(NB, E), cut(NB, E)
        pmax, padd = cut(NB * NG, 2), cut(NB * NG, 2)
        gscore = cut(NB * NG)
        gless = cut(NB, NG * NG)
        grank, gback = cut(NB, NG), cut(NB, NG)
        rank, back = cut(NB, E), cut(NB, E)
        comb, csum = cut(NB, E), cut(NB)
        less = cut(NB, E * E)
        th, inter = cut(2, T), cut(2, T)
        h1, h2 = cut(2, T), cut(2, T)

        at[0] = 0
        yg, x3 = cut(NB, D), cut(NB, D)
        cT = cut(DC, T)
        node = [cut(DC, T) for _ in range(NODES + 1)]
        keys = cut(DC, NB, STRIPS, S)
        qhT = cut(2, DC, T)
        aT = cut(DC, T)
        vx = cut(2, NB, D)
        vv = cut(NB, D)
        SLOTS = 3
        pr, pn = cut(SLOTS, STRIPS * S), cut(SLOTS, STRIPS * S)
        pT = cut(SLOTS, STRIPS * S)
        ynT = cut(DC, T)
        yn = cut(NB, D)
        res, yf = cut(NB, D), cut(NB, D)
        ident_h = cut(S // 2).bitcast(BF16)
        causal_h = cut(STRIPS * S // 2).bitcast(BF16)

        stats = sb("stats", [S, NB, 6])
        mv = sb("mv", [S, NB, 2])
        rs_v, rs_y, rs_t = sb("rs_v", [S, NB]), sb("rs_y", [S, NB]), sb("rs_t", [S, NB])
        RING = 8
        nmax = sb("nmax", [S, 1, NB])
        nbias = sb("nbias", [S, RING, NB])
        rsum, rinv = sb("rsum", [S, RING, NB]), sb("rinv", [S, RING, NB])

        attn_loaded = sem("attn_loaded")
        fuse_loaded = sem("fuse_loaded")
        fused = sem("fused")
        fused_copied = sem("fused_copied")
        loaded = sem("loaded")
        inputs_used = sem("inputs_used")
        vec = sem("vec")
        norm_ready = sem("norm_ready")
        turned = sem("turned")
        xnT_ready = sem("xnT_ready")
        q_ps, q_ready = sem("q_ps"), sem("q_ready")
        s_ps, max_ready = sem("s_ps"), sem("max_ready")
        exp_done = sem("exp_done")
        t_ps, t_copied = sem("t_ps"), sem("t_copied")
        o_ps, o_ready = sem("o_ps"), sem("o_ready")
        out_ps = sem("out_ps")
        bias_added = sem("bias_added")
        logit_ps, sig_ready = sem("logit_ps"), sem("sig_ready")
        comb_ready, combT_ps, combT_ready = sem("comb_ready"), sem("combT_ps"), sem("combT_ready")
        gu_ps, th_ready = sem("gu_ps"), sem("th_ready")
        gu_hi, gu_lo = sem("gu_hi"), sem("gu_lo")
        dn_hi, dn_lo = sem("dn_hi"), sem("dn_lo")
        in_hi, in_lo = sem("in_hi"), sem("in_lo")
        x_hi, x_lo = sem("x_hi"), sem("x_lo")
        h1_done, h2_done = sem("h1_done"), sem("h2_done")
        cb_ps, inter_ready, down_ps = sem("cb_ps"), sem("inter_ready"), sem("down_ps")
        k_ps, k_ready = sem("k_ps"), sem("k_ready")
        v_ps, v_ready = sem("v_ps"), sem("v_ready")
        k_shared = sem("k_shared")
        e_ps, e_ready = sem("e_ps"), sem("e_ready")
        rinv_ready, normed = sem("rinv_ready"), sem("normed")
        x3_ready, node_ready = sem("x3_ready"), sem("node_ready")
        fin_ps, fin_ready = sem("fin_ps"), sem("fin_ready")
        zeroed = sem("zeroed")
        scaled = sem("scaled")
        result = sem("result")
        x_loaded = sem("x_loaded")
        x1_free = sem("x1_free")
        wo_loaded, edge_q_loaded = sem("wo_loaded"), sem("edge_q_loaded")
        rest_loaded = sem("rest_loaded")
        stored = sem("stored")
        go_pe, go_act, go_dve, go_pool = sem("go_pe"), sem("go_act"), sem("go_dve"), sem("go_pool")
        counts = {}
        block = ctx.enter_context(nc.Block())

        PROJECTION_BANKS = (4, 5, 7)

        def projection_bank(name, r):
            return bank[PROJECTION_BANKS[BANK_ORDER.index((name, r)) % 3]]

        def nth(name, r, alone):
            return 1 if alone else [q for what, q in ORDER if what == name].index(r) + 1

        def nth_node(r, alone):
            return 1 if alone else NODE_OUTS.index(r) + 1

        @block.sync
        def _(sp):
            def release(*engines):
                sp.sem_clear(range(attn_loaded.num, x1_free.num + 1))
                for s in engines or (go_pe, go_act, go_dve, go_pool):
                    sp.sem_inc(s, 1)

            def load(dst, src, done):
                counts[done.name] = counts.get(done.name, 0) + 16
                sp.dma_start(dst, src).then_inc(done, 16)

            def to_all(dst, src):
                load(dst, src.partition_broadcast(dst.shape[0]), attn_loaded)

            load(wk0[:], rows(a["L0_xattn_Wk"]), attn_loaded)
            load(wq0[:], rows(a["L0_xattn_Wq"]), attn_loaded)
            load(wv0[:], rows(a["L0_xattn_Wv"]), attn_loaded)
            load(wo0[:], rows(a["L0_xattn_WoT"]), attn_loaded)
            sp.dma_start(xg[0:S], a["x"][0:T, :].rearrange("(b s) d -> s b d", s=S)).then_inc(x_loaded, 16)
            load(ident[:], a["c_ident"], attn_loaded)
            load(causal[:], a["c_causal"], attn_loaded)
            load(half_mask[:], a["c_half_mask"], attn_loaded)
            to_all(earlier[:], a["c_earlier"])
            to_all(later_n[:], a["c_later_n"])
            to_all(gbias[:], a["L0_ffn_gate_bias"])
            to_all(bias0[:], a["L0_xattn_bo"])
            to_all(bo1[:], a["L1_xattn_bo"])
            to_all(ln_g[:], a["L1_ffn_ln_g"])
            to_all(ln_b[:], a["L1_ffn_ln_b"])
            to_all(ewc[:].rearrange("p n k -> p (n k)"), a["L1_ffn_ew"].rearrange("n k -> (n k)"))
            to_all(actw[:], a["L1_ffn_act_w"])
            for dst, name in ((raw_bq0, "L0_xattn_bq"), (raw_bv0, "L0_xattn_bv"), (bq1, "L1_xattn_bq"),
                              (bk1, "L1_xattn_bk"), (bv1, "L1_xattn_bv")):
                load(dst[:], a[name], attn_loaded)
            for i in range(NODES):
                for k in range(3):
                    load(be_in[:, k, i], a["L1_ffn_beT"][DAG[i][k][1]], attn_loaded)
            for i in range(NODES):
                load(weT[:, i], rows(a["L1_ffn_WeT"][DAG[i][1][1]]), fuse_loaded)
                load(weT[:, NODES + i], rows(a["L1_ffn_WeT"][DAG[i][2][1]]), fuse_loaded)
                load(wkv[:, i], rows(a["L1_ffn_Wk"][i]), fuse_loaded)
                load(wkv[:, NODES + i], rows(a["L1_ffn_Wv"][i]), fuse_loaded)
            load(gatek[:], rows(a["L0_ffn_gate_kernel"]), rest_loaded)
            for c in range(DC):
                chunk = slice(c * P, (c + 1) * P)
                load(w_gate[:, 2:, c], a["L0_ffn_w_gate"][:, chunk, :].rearrange("e p m -> p e m"), rest_loaded)
                load(w_up[:, 2:, c], a["L0_ffn_w_up"][:, chunk, :].rearrange("e p m -> p e m"), rest_loaded)
                load(w_gate[:, 0:2, c], a["L0_ffn_sw_gate"][chunk, :].rearrange("p (e m) -> p e m", m=M), rest_loaded)
                load(w_up[:, 0:2, c], a["L0_ffn_sw_up"][chunk, :].rearrange("p (e m) -> p e m", m=M), rest_loaded)
            load(w_down[:, 2:], a["L0_ffn_w_down"].rearrange("e p n -> p e n"), rest_loaded)
            load(w_down[:, 0:2], rows(a["L0_ffn_sw_down"]), rest_loaded)
            load(x_wq[:], rows(a["L1_xattn_WqT"]), rest_loaded)
            load(x_wk[:], rows(a["L1_xattn_WkT"]), rest_loaded)
            load(x_wv[:], rows(a["L1_xattn_WvT"]), rest_loaded)
            load(x_wo[:], rows(a["L1_xattn_WoT"]), rest_loaded)

            def load_x(g):
                sp.dma_start(xg[0:S], a["x"][bass.ds(g * T, T), :].rearrange("(b s) d -> s b d", s=S)).then_inc(x_loaded, 16)

            def load_context(g):
                for b in range(NB):
                    sp.dma_start(ctxg[0:CT, b], a["ctx"][bass.ds((g * NB + b) * SC, SC), :].rearrange(
                        "(t p) d -> p t d", p=CT)).then_inc(loaded, 16)
                sp.dma_start(ctxT[:], a["ctxT"][:, bass.ds(g * NB * SC, NB * SC)].rearrange(
                    "(c p) s -> p c s", p=P)).then_inc(loaded, 16)

            def wait_stored():
                sp.wait_ge(stored, 16)
                sp.sem_clear(stored)

            LOADS = 16 * (1 + NB)
            sp.wait_ge(result, 1)
            release(go_pe, go_act, go_pool)
            load_context(0)
            sp.wait_ge(loaded, LOADS)
            sp.wait_ge(q_ready, DC)
            sp.wait_ge(bias_added, 1)
            sp.wait_ge(rest_loaded, counts[rest_loaded.name])
            release()

            def group1(g, first, last):
                if last:
                    sp.sem_inc(x_loaded, 16)
                else:
                    load_x(g + 1)
                if not first:
                    wait_stored()
                sp.sem_inc(x1_free, 1)
                if not last:
                    sp.wait_ge(inputs_used, 1)
                    load_context(g + 1)
                sp.wait_ge(bias_added, 1)
                if not last:
                    sp.wait_ge(loaded, LOADS)
                sp.wait_ge(result, 2)
                if not last:
                    release()
                sp.dma_start(x2_dram[bass.ds(g * T, T), :].rearrange("(b s) d -> s b d", s=S), x1[0:S]).then_inc(stored, 16)

            group1(0, True, False)
            with sp.Fori(1, G - 1) as g:
                group1(g, False, False)
            group1(G - 1, False, True)
            wait_stored()

            def load_group2(g):
                sp.dma_start(yg[0:S], x2_dram[bass.ds(g * T, T), :].rearrange("(b s) d -> s b d", s=S)).then_inc(loaded, 16)
                for c in range(DC):
                    sp.dma_start(cT[:, c].rearrange("p (b s) -> p b s", b=NB),
                                 a["ctxT"][c * P:(c + 1) * P, bass.ds(g * NB * SC, NB * SC)].rearrange(
                                     "p (b s) -> p b s", b=NB)[:, :, 0:S]).then_inc(loaded, 16)

            release()
            LOADS2 = 16 * (1 + DC)
            load_group2(0)
            for i in range(NODES):
                sp.dma_start(f_wo[:, i], rows(a["L1_ffn_Wo"][i])).then_inc(wo_loaded, 16)
            for i in range(NODES):
                sp.dma_start(f_edge[:, i], rows(a["L1_ffn_We"][DAG[i][0][1]])).then_inc(edge_q_loaded, 16)
                sp.dma_start(f_wq[:, i], rows(a["L1_ffn_Wq"][i])).then_inc(edge_q_loaded, 16)
            sp.wait_ge(zeroed, 2)
            for s in (k_ready, v_ready, q_ready):
                sp.wait_ge(s, 1)
            release()

            def store_group2(g):
                sp.wait_ge(result, 1)
                sp.dma_start(out[bass.ds(g * T, T), :].rearrange("(b s) d -> s b d", s=S), yf[0:S]).then_inc(stored, 16)
                wait_stored()

            def group2(g, first, last):
                sp.wait_ge(inputs_used, 1)
                if last:
                    sp.sem_inc(loaded, LOADS2)
                else:
                    load_group2(g + 1)
                if first:
                    sp.wait_ge(result, 1)
                else:
                    store_group2(g - 1)
                for s, name in ((k_ready, "keys"), (v_ready, "values"), (q_ready, "queries")):
                    sp.wait_ge(s, nth(name, -1, False))
                sp.wait_ge(o_ready, WINDOWS)
                release()

            group2(0, True, False)
            with sp.Fori(1, G - 1) as g:
                group2(g, False, False)
            group2(G - 1, False, True)
            store_group2(G - 1)

        @block.tensor
        def _(pe):
            mm = nc.tensor.matmul

            pe.wait_ge(attn_loaded, counts[attn_loaded.name])
            jobs = [(wq0, wk0), (wv0, wo0)] + [(weT[:, i], wkv[:, i]) for i in range(2 * NODES)]
            for i, (lhsT, rhs) in enumerate(jobs):
                if i == 2:
                    pe.wait_ge(fuse_loaded, counts[fuse_loaded.name])
                if i >= 8:
                    pe.wait_ge(fused_copied, i - 7)
                for o in range(DC):
                    for c in range(DC):
                        last = mm(bank[i % 8][:, o * D:(o + 1) * D], lhsT[:, c, o * P:(o + 1) * P], rhs[:, c, :],
                                  start=(c == 0), stop=(c == DC - 1))
                last.then_inc(fused, 1)
            i = len(jobs)
            pe.wait_ge(fused_copied, i - 7)
            for o in range(DC):
                for c in range(DC):
                    mm(bank[i % 8][:, o:o + 1], wk0[:, c, o * P:(o + 1) * P], raw_bq0[:, c:c + 1],
                       start=(c == 0), stop=(c == DC - 1))
            for k in range(2 * NODES):
                for o in range(DC):
                    for c in range(DC):
                        last = mm(bank[i % 8][:, 2 + 2 * k + o:3 + 2 * k + o], wkv[:, k, c, o * P:(o + 1) * P],
                                  be_in[:, 1 + k // NODES, k % NODES, c:c + 1], start=(c == 0), stop=(c == DC - 1))
            last.then_inc(fused, 1)
            i += 1
            pe.wait_ge(fused_copied, i - 7)
            for c in range(DC):
                last = mm(bank[i % 8][0:S, 0:D], raw_bv0[:, c:c + 1].to_broadcast([P, S]), wo0[:, c, :],
                          start=(c == 0), stop=(c == DC - 1))
            last.then_inc(fused, 1)

            def go():
                pe.wait_ge(go_pe, 1)
                pe.sem_clear(go_pe)

            def project(bank0, w, xT, done):
                for o in range(DC):
                    for c in range(DC):
                        last = mm(bank[bank0 + o][:, 0:T], w[:, c, o * P:(o + 1) * P], xT[:, c, :],
                                  start=(c == 0), stop=(c == DC - 1))
                    last.then_inc(done, 1)

            def next_queries(bank0, alone=False):
                for b in range(NB):
                    if not alone:
                        pe.wait_ge(norm_ready, b + 1)
                    for c in range(DC):
                        col = c * TH + b % HB * S
                        last = nc.tensor.transpose(bank[bank0 + b // HB][:, col:col + S], xnext[0:S, b, c * P:(c + 1) * P],
                                                   ident[0:S, 0:S])
                    if b % HB == HB - 1:
                        last.then_inc(turned, 1)
                pe.wait_ge(xnT_ready, 2)
                project(bank0 + 2, score0, xnT, q_ps)

            go()
            next_queries(4, alone=True)
            with pe.Fori(0, G):
                go()
                for b in range(NB):
                    for c in range(DC):
                        last = mm(bank[4 + b][0:S, 0:SC], qT[:, c, b * S:(b + 1) * S],
                                  ctxT[:, c, b * SC:(b + 1) * SC], start=(c == 0), stop=(c == DC - 1))
                    last.then_inc(s_ps, 1)
                for i in range(NB + 1):
                    if i < NB:
                        pe.wait_ge(exp_done, i + 1)
                        if i >= 2:
                            pe.wait_ge(t_copied, i - 1)
                        for t in range(NT):
                            last = nc.tensor.transpose(bank[i % 2][0:CT, t * S:(t + 1) * S],
                                                       pr0[0:S, i, t * CT:(t + 1) * CT], ident[0:S, 0:S])
                        last.then_inc(t_ps, 1)
                    if i >= 1:
                        b = i - 1
                        pe.wait_ge(t_copied, b + 1)
                        for c in range(DC):
                            for t in range(NT):
                                col = c * TH + b % HB * S
                                last = mm(bank[2 + b // HB][:, col:col + S], ctxg[0:CT, b, t, c * P:(c + 1) * P],
                                          pT0[0:CT, b % 2, t * S:(t + 1) * S], start=(t == 0), stop=(t == NT - 1))
                        last.then_inc(o_ps, 1)
                for b in range(NB):
                    pe.wait_ge(o_ready, b // HB + 1)
                    for c in range(DC):
                        last = mm(bank[b // 2][0:S, (b % 2) * D:(b % 2 + 1) * D], oT[:, c, b * S:(b + 1) * S],
                                  value0[:, c, :], start=(c == 0), stop=(c == DC - 1))
                    if b % 2:
                        last.then_inc(out_ps, 1)
                next_queries(4)
                pe.wait_ge(q_ready, DC)
                for b in range(NB):
                    pe.wait_ge(norm_ready, NB + b + 1)
                    for c in range(DC):
                        col = c * TH + b % HB * S
                        last = nc.tensor.transpose(bank[b // HB][:, col:col + S], xn[0:S, b, c * P:(c + 1) * P],
                                                   ident[0:S, 0:S])
                    if b % HB == HB - 1:
                        last.then_inc(turned, 1)
                for b in range(NB):
                    pe.wait_ge(xnT_ready, 2 + b // HB + 1)
                    for c in range(DC):
                        last = mm(bank[2][0:S, b * E:(b + 1) * E], xnT[:, c, b * S:(b + 1) * S], gatek[:, c, :],
                                  start=(c == 0), stop=(c == DC - 1))
                last.then_inc(logit_ps, 1)
                def down(k):
                    pe.wait_ge(dn_lo, k + 1)
                    pe.wait_ge(in_lo, k + 1)
                    for b in range(NB):
                        for i, (hl, whl) in enumerate(((0, 0), (0, 1), (1, 0))):
                            last = mm(bank[b // 2][0:S, (b % 2) * D:(b % 2 + 1) * D],
                                      inr[:, k % 2, hl, b * S:(b + 1) * S], w_dn[:, k % 2, whl, :],
                                      start=(k == 0 and b % 2 == 0 and i == 0), stop=(k == E + 1 and i == 2),
                                      skip_group_check=True)
                    last.then_inc(down_ps, 1)

                pe.wait_ge(x_lo, 2)
                for k in range(E + 4):
                    if k < E + 2:
                        if k >= 2:
                            pe.wait_ge(h2_done, k - 1)
                        pe.wait_ge(gu_lo, k + 1)
                        for w, bk in ((0, 4), (1, 6)):
                            for c in range(DC):
                                for i, (hl, xhl) in enumerate(((0, 0), (0, 1), (1, 0))):
                                    last = mm(bank[bk + k % 2][:, 0:T], w_gu[:, k % 2, w, c, hl, :], xr[:, c, xhl, :],
                                              start=(c == 0 and i == 0), stop=(c == DC - 1 and i == 2))
                        last.then_inc(gu_ps, 1)
                    if k == 3:
                        pe.wait_ge(comb_ready, 1)
                        for b in range(NB):
                            last = nc.tensor.transpose(bank[3][0:E, b * S:(b + 1) * S], comb[0:S, b, :], ident[0:S, 0:S])
                        last.then_inc(combT_ps, 1)
                    if k == 3:
                        down(k - 2)
                    if 2 <= k - 1 < E + 2:
                        pe.wait_ge(combT_ready, 1)
                        if k >= 5:
                            pe.wait_ge(inter_ready, k - 4)
                        for hl in range(2):
                            last = mm(bank[2 + (k - 1) % 2][:, 0:T], ident_e[:, k - 3:k - 2].to_broadcast([E, P]),
                                      combr[:, hl, :], start=(hl == 0), stop=(hl == 1))
                        last.then_inc(cb_ps, 1)
                    if k >= 2 and k != 3:
                        down(k - 2)

            readouts = []

            def next_bank(name, r, s, n):
                if len(readouts) >= 3:
                    pe.wait_ge(*readouts[-3])
                readouts.append((s, n))
                return projection_bank(name, r)

            def project_half(bk, w, xT, h, done):
                for o in range(DC):
                    for i in range(DC):
                        last = mm(bk[:, o * TH:(o + 1) * TH], w[:, i, o * P:(o + 1) * P], xT[:, i, h * TH:(h + 1) * TH],
                                  start=(i == 0), stop=(i == DC - 1))
                last.then_inc(done, 1)

            def project_batch(bk, xT, w, h, b):
                for i in range(DC):
                    last = mm(bk[0:S, b * D:(b + 1) * D], xT[:, i, h * TH + b * S:h * TH + (b + 1) * S], w[:, i, :],
                              start=(i == 0), stop=(i == DC - 1))
                return last

            def piece(name, r, alone=False):
                h = 1 - r % 2
                c = (r - 1) // 2
                n = nth(name, r, alone)
                if name == "keys":
                    bk = next_bank(name, r, k_ready, n)
                    w, src = (x_wk, cT) if r <= 0 else (f_kk[:, c], node[DAG[c][1][0] + 1])
                    project_half(bk, w, src, h, k_ps)
                elif name in ("values", "values_end"):
                    b = 0
                    if name == "values":
                        bk = next_bank(name, r, v_ready, n)
                    else:
                        b, bk = 1, projection_bank("values", r)
                    w, src = (x_wv, cT) if r <= 0 else (f_vv[:, c], node[DAG[c][2][0] + 1])
                    last = project_batch(bk, src, w, h, b)
                    if b == 1:
                        last.then_inc(v_ps, 1)
                elif name == "turn":
                    bk = next_bank(name, r, xnT_ready, n)
                    for b in range(HB):
                        if r:
                            pe.wait_ge(norm_ready, (0 if alone else NORMS[r]) + b + 1)
                        for i in range(DC):
                            last = nc.tensor.transpose(bk[:, i * TH + b * S:i * TH + (b + 1) * S],
                                                       yn[0:S, h * HB + b, i * P:(i + 1) * P], ident[0:S, 0:S])
                    last.then_inc(turned, 1)
                elif name == "queries":
                    bk = next_bank(name, r, q_ready, n)
                    if r <= 0:
                        pe.wait_ge(xnT_ready, nth("turn", r, alone))
                        project_half(bk, x_wq, ynT, h, q_ps)
                    else:
                        pe.wait_ge(e_ready, nth("edge", r, alone))
                        project_half(bk, f_wq[:, c], node[c + 1], h, q_ps)
                elif name == "edge":
                    bk = next_bank(name, r, e_ready, n)
                    if r <= 2:
                        pe.wait_ge(xnT_ready, nth("turn", r, alone))
                    else:
                        pe.wait_ge(node_ready, nth_node(r, alone))
                    project_half(bk, f_edge[:, c], node[c], h, e_ps)
                elif name == "out":
                    if r < LAST:
                        pe.wait_ge(o_ready, r)
                    if r <= 2:
                        bk = next_bank(name, r, x3_ready, r)
                        for b in range(HB):
                            last = project_batch(bk, aT, x_wo, h, b)
                        last.then_inc(out_ps, 1)
                    else:
                        bk = next_bank(name, r, node_ready, nth_node(r, alone))
                        project_half(bk, f_wo[:, c - 1], aT, h, out_ps)
                elif name == "final":
                    bk = next_bank(name, r, fin_ready, r - LAST + 2)
                    if r == LAST:
                        pe.wait_ge(node_ready, 1)
                    for b in range(HB):
                        for i in range(DC):
                            last = nc.tensor.transpose(bk[0:S, b * D + i * P:b * D + (i + 1) * P],
                                                       node[NODES][:, i, h * TH + b * S:h * TH + (b + 1) * S], ident[:, :])
                    last.then_inc(fin_ps, 1)

            def scores(w, n, c, b, par):
                if n >= 3:
                    pe.wait_ge(exp_done, n - 2)
                last = mm(bank[n % 3][0:S, 0:T], qhT[:, par, c, b * S:(b + 1) * S],
                          keys[:, c, b].rearrange("p j s -> p (j s)"), start=True, stop=(w >= 2))
                if w < 2:
                    last = mm(bank[n % 3][0:S, 0:T], ident_h[0:S],
                              causal_h[0:S], start=False, stop=True)
                last.then_inc(s_ps, 1)

            def turn_probs(n):
                pe.wait_ge(normed, n + 1)
                if n:
                    pe.wait_ge(t_copied, n)
                for j in range(STRIPS):
                    last = nc.tensor.transpose(bank[3][0:S, j * S:(j + 1) * S],
                                               pn[0:S, n % SLOTS, j * S:(j + 1) * S], ident[0:S, 0:S])
                last.then_inc(t_ps, 1)

            def weigh(w, n, c, b, par):
                pe.wait_ge(t_copied, n + 1)
                for j in range(STRIPS):
                    col = c * P + 32 * j
                    last = mm(bank[6][32 * j:32 * j + 32, c * TH + b % HB * S:c * TH + (b % HB + 1) * S],
                              vx[0:S, par, b, col:col + 32] if w < 2 else vv[0:S, b, col:col + 32],
                              pT[0:S, n % SLOTS, j * S:(j + 1) * S], start=(par == 0), stop=(par == 1 or w >= 2))
                last.then_inc(o_ps, 1)

            go()
            pe.wait_ge(loaded, 16 * (1 + DC))
            for name in ("keys", "values", "values_end", "turn", "queries"):
                if name == "values":
                    pe.wait_ge(k_ready, 1)
                readouts.clear()
                piece(name, -1, alone=True)
            pe.wait_ge(wo_loaded, 16 * NODES)
            with pe.Fori(0, G):
                readouts.clear()
                go()
                for w in range(WINDOWS):
                    sets = SETS[w]
                    if w == 1:
                        pe.wait_ge(edge_q_loaded, 32 * NODES)
                    if w:
                        pe.wait_ge(k_ready, w)
                        pe.wait_ge(q_ready, w)
                        if w - 1 in SHARED_KEYS:
                            pe.wait_ge(k_shared, SHARED_KEYS.index(w - 1) + 1)
                    for i in range(steps(w)):
                        t, o = i - lag(w), i - lag(w) - 1
                        if i == 0 and w:
                            turn_probs(SETS[w - 1][-1][0])
                        if i < len(sets):
                            scores(w, *sets[i])
                        if o == 0 and w:
                            pe.wait_ge(v_ready, w)
                            pe.wait_ge(o_ready, w)
                        if o >= 0:
                            weigh(w, *sets[o])
                        if i == 1 and w:
                            weigh(w - 1, *SETS[w - 1][-1])
                        if 0 <= t < len(sets) - 1:
                            turn_probs(sets[t][0])
                        for name, r in pieces(w).get(i, []):
                            piece(name, r)
                turn_probs(SETS[-1][-1][0])
                weigh(WINDOWS - 1, *SETS[-1][-1])
            go()
            readouts.clear()
            piece("final", LAST - 1, alone=True)
            piece("out", LAST, alone=True)
            piece("final", LAST, alone=True)

        @block.scalar
        def _(act):
            def go():
                act.wait_ge(go_act, 1)
                act.sem_clear(go_act)

            def halves(bk):
                return bk[:, 0:T].rearrange("p (c s) -> p c s", c=DC)

            def take_turned(k, dst, bank0):
                for h in range(2):
                    act.wait_ge(turned, 2 * k + h + 1)
                    nc.scalar.activation(dst[:, :, h * TH:(h + 1) * TH], halves(bank[bank0 + h]),
                                         ACT.Identity).then_inc(xnT_ready, 1)

            def split_gu(k):
                for i, w in enumerate((w_gate, w_up)):
                    last = nc.scalar.activation(w_gu[:, k % 2, i, :, 0, :], w[:, k], ACT.Identity)
                last.then_inc(gu_hi, 1)

            def split_inter(k):
                if k < 2:
                    act.wait_ge(h2_done, k + 1)
                else:
                    act.wait_ge(inter_ready, k - 1)
                    act.wait_ge(down_ps, k - 1)
                nc.scalar.activation(inr[:, k % 2, 0, :], inter[:, k % 2, :], ACT.Identity).then_inc(in_hi, 1)

            def take_next_queries():
                take_turned(0, xnT, 4)
                for o in range(DC):
                    act.wait_ge(q_ps, o + 1)
                    nc.scalar.activation(qT[:, o, :], bank[6 + o][:, 0:T], ACT.Identity,
                                         bias=bq0[:, o:o + 1]).then_inc(q_ready, 1)

            go()
            take_next_queries()
            with act.Fori(0, G):
                go()
                split_gu(0)
                split_gu(1)
                for b in range(NB):
                    act.wait_ge(max_ready, b + 1)
                    nc.scalar.activation(pr0[0:S, b, :], bank[4 + b][0:S, 0:SC], ACT.Exp, bias=nbias[:, 0, b:b + 1],
                                         scale=float(D) ** -0.5, accum_out=rsum[:, 0, b:b + 1]).then_inc(exp_done, 1)
                for h in range(2):
                    act.wait_ge(o_ps, HB * (h + 1))
                    nc.scalar.activation(oT[:, :, h * TH:(h + 1) * TH], halves(bank[2 + h]), ACT.Identity).then_inc(o_ready, 1)
                take_next_queries()
                take_turned(1, xnT, 0)
                for h in range(2):
                    nc.scalar.activation(xr[:, :, 0, h * TH:(h + 1) * TH], halves(bank[h]), ACT.Identity).then_inc(x_hi, 1)
                act.wait_ge(logit_ps, 1)
                nc.scalar.activation(sig[0:S], bank[2][0:S, 0:NB * E].rearrange("p (b e) -> p b e", b=NB),
                                     ACT.Tanh, scale=0.5).then_inc(sig_ready, 1)
                for k in range(E + 2):
                    act.wait_ge(gu_ps, k + 1)
                    if k >= 2:
                        act.wait_ge(h1_done, k - 1)
                    nc.scalar.activation(th[:, k % 2, :], bank[4 + k % 2][:, 0:T], ACT.Tanh,
                                         scale=0.5).then_inc(th_ready, 1)
                    if k + 2 < E + 2:
                        split_gu(k + 2)
                    if k >= 1:
                        split_inter(k - 1)
                    if k >= 2:
                        act.wait_ge(down_ps, k - 1)
                    nc.scalar.activation(w_dn[:, k % 2, 0, :], w_down[:, k], ACT.Identity).then_inc(dn_hi, 1)
                split_inter(E + 1)

            def take_keys(r, strips, alone=False):
                h, c = 1 - r % 2, (r - 1) // 2
                bk = projection_bank("keys", r)
                act.wait_ge(k_ps, nth("keys", r, alone))
                for j, o in [(j, o) for j in strips for o in range(DC)]:
                    p = slice(32 * j, 32 * j + 32)
                    last = nc.scalar.activation(
                        keys[p, o, h * HB:(h + 1) * HB, j, :], bk[p, o * TH:(o + 1) * TH].rearrange("p (b s) -> p b s", b=HB),
                        ACT.Identity, bias=bk1[p, o:o + 1] if r <= 0 else be_kv[p, 0, c, o:o + 1],
                        scale=1.0 if r <= 0 else ewc[p, c, 1:2])
                if strips[-1] == STRIPS - 1 or r in SHARED_KEYS:
                    last.then_inc(k_ready, 1)

            def take_values(r):
                h, c = 1 - r % 2, (r - 1) // 2
                act.wait_ge(v_ps, nth("values", r, False))
                nc.scalar.activation(vv[0:S, h * HB:(h + 1) * HB, :],
                                     projection_bank("values", r)[0:S, :].rearrange("p (b d) -> p b d", b=HB),
                                     ACT.Identity, scale=ewc[0:S, c, 2:3]).then_inc(v_ready, 1)

            def take_final(r):
                h = 1 - r % 2
                act.wait_ge(fin_ps, r - LAST + 2)
                nc.scalar.activation(yf[0:S, h * HB:(h + 1) * HB, :],
                                     projection_bank("final", r)[0:S, :].rearrange("p (b d) -> p b d", b=HB),
                                     ACT.Identity).then_inc(fin_ready, 1)

            def take_queries(r, alone=False):
                h = 1 - r % 2
                bk = projection_bank("queries", r)
                act.wait_ge(q_ps, nth("queries", r, alone))
                for o in range(DC):
                    for par in range(2):
                        last = nc.scalar.activation(qhT[:, par, o, h * TH:(h + 1) * TH], bk[:, o * TH:(o + 1) * TH],
                                                    ACT.Identity, scale=half_mask[:, par:par + 1],
                                                    bias=bq1_half[:, par, o:o + 1])
                last.then_inc(q_ready, 1)

            go()
            act.wait_ge(zeroed, 1)
            take_keys(-1, range(STRIPS), alone=True)
            take_queries(-1, alone=True)
            with act.Fori(0, G):
                go()
                for w in range(WINDOWS):
                    for i in range(steps(w) + 1):
                        if i < len(SETS[w]):
                            n = SETS[w][i][0]
                            act.wait_ge(max_ready, n + 1)
                            if n >= SLOTS:
                                act.wait_ge(normed, n - SLOTS + 1)
                            for j in range(STRIPS):
                                last = nc.scalar.activation(
                                    pr[0:S, n % SLOTS, j * S:(j + 1) * S], bank[n % 3][0:S, j * S:(j + 1) * S], ACT.Exp,
                                    bias=nbias[:, n % RING, j:j + 1], accum_out=rsum[:, n % RING, j:j + 1])
                            last.then_inc(exp_done, 1)
                        if w == 0 and 4 <= i < 4 + STRIPS:
                            take_keys(0, [i - 4])
                        due = pieces(w).get(0, []) if i == 2 else []
                        due = due + (pieces(w).get(i - 1, []) if i >= 2 else [])
                        for name, r in due:
                            if name == "keys" and r:
                                take_keys(r, range(2) if r in SHARED_KEYS else range(STRIPS))
                            elif name == "values_end" and r > 0:
                                take_values(r)
                            elif name == "final":
                                take_final(r)
                            elif name == "queries" and r <= 0:
                                take_queries(r)
            go()
            take_final(LAST - 1)
            take_final(LAST)

        @block.vector
        def _(dve):
            V = nc.vector
            chain = [0]

            def link(ins):
                chain[0] += 1
                ins.then_inc(vec, 1)
                dve.wait_ge(vec, chain[0])

            def go():
                dve.wait_ge(go_dve, 1)
                dve.sem_clear(go_dve)
                chain[0] = normalized[0] = 0

            normalized = [0]

            def norm_stats(src, batches=None):
                n = src.shape[1]
                if normalized[0] and batches is None:
                    dve.wait_ge(norm_ready, normalized[0])
                for b in batches or range(n):
                    last = V.bn_stats(stats[:, b, :], src[0:S, b, :])
                link(last)
                if batches is None:
                    norm_means(n)

            def norm_means(n):
                for b in range(n):
                    last = V.bn_aggr(mv[:, b, :], stats[:, b, :])
                link(last)

            def norm_guess(eps, n):
                v, y = rs_v[:, 0:n], rs_y[:, 0:n]
                link(V.tensor_scalar(v, mv[:, 0:n, 1], eps, None, ALU.add))
                link(V.tensor_single_scalar(y.bitcast(I32), v.bitcast(I32), 1, ALU.arith_shift_right))
                link(V.tensor_scalar(y.bitcast(I32), y.bitcast(I32), -1.0, float(0x5F3759DF), ALU.mult, ALU.add))

            def norm_newton(n):
                v, y, t = rs_v[:, 0:n], rs_y[:, 0:n], rs_t[:, 0:n]
                link(V.tensor_tensor(t, v, y, ALU.mult))
                link(V.scalar_tensor_tensor(t, t, -0.5, y, ALU.mult, ALU.mult))
                link(V.scalar_tensor_tensor(y, t, 1.5, y, ALU.add, ALU.mult))

            def norm_rsqrt(eps, n):
                norm_guess(eps, n)
                for _ in range(3):
                    norm_newton(n)

            def norm_apply(dst, src, batches=None):
                batches = batches or range(src.shape[1])
                for b in batches:
                    V.tensor_scalar(dst[0:S, b, :], src[0:S, b, :], mv[:, b, 0:1], rs_y[:, b:b + 1],
                                    ALU.subtract, ALU.mult).then_inc(norm_ready, 1)
                normalized[0] += len(batches)

            def norm_part(dst, src, eps, part):
                if part == 0:
                    dve.wait_ge(norm_ready, normalized[0])
                if part < 2:
                    norm_stats(src, range(part * HB, (part + 1) * HB))
                elif part == 2:
                    norm_means(NB)
                elif part == 3:
                    norm_guess(eps, NB)
                elif part < 7:
                    norm_newton(NB)
                else:
                    norm_apply(dst, src, range((part - 7) * HB, (part - 6) * HB))

            def layernorm(dst, src, eps):
                norm_stats(src)
                norm_rsqrt(eps, src.shape[1])
                norm_apply(dst, src)

            dve.wait_ge(x_loaded, 16)
            layernorm(xnext, xg, L0_EPS)
            dve.wait_ge(attn_loaded, counts[attn_loaded.name])
            V.tensor_copy(ident_e[:], ident[0:E, 0:E])
            link(V.tensor_scalar(half_mask[:], half_mask[:], float(XD) ** -0.5, None, ALU.mult))
            for par in range(2):
                V.tensor_scalar(bq1_half[:, par, :], bq1[:], half_mask[:, par:par + 1], None, ALU.mult)
            V.tensor_tensor(be_q[:], be_in[:, 0], ewc[:, :, 0:1].to_broadcast([P, NODES, DC]), ALU.mult)
            dsts = [score0[:], value0[:]] + [f_kk[:, i] for i in range(NODES)] + [f_vv[:, i] for i in range(NODES)]
            for i, dst in enumerate(dsts):
                dve.wait_ge(fused, i + 1)
                V.tensor_copy(dst, bank[i % 8][:, :].rearrange("p (c n) -> p c n", c=DC)).then_inc(fused_copied, 1)
            i = len(dsts)
            dve.wait_ge(fused, i + 1)
            V.tensor_copy(bq0[:], bank[i % 8][:, 0:DC])
            for k in range(2):
                last = V.tensor_tensor(be_kv[:, k], bank[i % 8][:, 2 + k * NODES * DC:2 + (k + 1) * NODES * DC].rearrange(
                    "p (n c) -> p n c", c=DC), ewc[:, :, 1 + k:2 + k].to_broadcast([P, NODES, DC]), ALU.mult)
            last.then_inc(fused_copied, 1)
            dve.wait_ge(fused, i + 2)
            V.tensor_tensor(bias0[:], bank[(i + 1) % 8][0:S, 0:D], bias0[:], ALU.add).then_inc(result, 1)

            s64 = choice[0:S]

            def compare(v, n, less_):
                L = less_[0:S].rearrange("p b (i j) -> p b i j", i=n)
                for b in range(NB):
                    last = V.tensor_tensor(L[:, b], v[:, b, :].unsqueeze(1).to_broadcast([S, n, n]),
                                           v[:, b, :].unsqueeze(2).to_broadcast([S, n, n]), ALU.is_ge)
                link(last)
                e_ = earlier[:].rearrange("p (i j) -> p i j", i=E)[:, 0:n, 0:n]
                for b in range(NB):
                    last = V.tensor_tensor(L[:, b], L[:, b], e_, ALU.mult)
                link(last)

            def ranks(n, less_, rank_, back_):
                L = less_[0:S].rearrange("p b (i j) -> p b i j", i=n)
                V.tensor_reduce(rank_[0:S], L, axis=AX, op=ALU.add)
                link(V.tensor_reduce(back_[0:S], L.rearrange("p b i j -> p b j i"), axis=AX, op=ALU.add))
                link(V.tensor_tensor(rank_[0:S], rank_[0:S], back_[0:S], ALU.subtract))
                link(V.tensor_tensor(rank_[0:S], rank_[0:S],
                                     later_n[:, E - n:E].unsqueeze(1).to_broadcast([S, NB, n]), ALU.add))

            def route_groups():
                link(V.tensor_scalar(s64, sig[0:S], 0.5, 0.5, ALU.mult, ALU.add))
                link(V.tensor_tensor(s64, s64, gbias[:].unsqueeze(1).to_broadcast([S, NB, E]), ALU.add))
                quads = s64.rearrange("p b (g h w) -> p (b g) h w", g=NG, h=2)
                V.tensor_tensor(pmax[0:S], quads[:, :, :, 0], quads[:, :, :, 1], ALU.max)
                link(V.tensor_tensor(padd[0:S], quads[:, :, :, 0], quads[:, :, :, 1], ALU.add))
                link(V.tensor_tensor(gscore[0:S], pmax[0:S, :, 0], pmax[0:S, :, 1], ALU.add))
                for h in range(2):
                    link(V.tensor_tensor(gscore[0:S], gscore[0:S], padd[0:S, :, h], ALU.max))

                compare(gscore[0:S].rearrange("p (b g) -> p b g", b=NB), NG, gless)
                ranks(NG, gless, grank, gback)
                link(V.tensor_single_scalar(grank[0:S], grank[0:S], 1.5, ALU.is_lt))
                link(V.tensor_tensor(s64.rearrange("p b (g w) -> p (b g) w", g=NG), s64.rearrange("p b (g w) -> p (b g) w", g=NG),
                                     grank[0:S].rearrange("p b g -> p (b g)").unsqueeze(2).to_broadcast([S, NB * NG, GE]), ALU.mult))

            def compare_experts():
                compare(s64, E, less)

            def route_experts():
                ranks(E, less, rank, back)
                link(V.scalar_tensor_tensor(comb[0:S], rank[0:S], 3.5, s64, ALU.is_lt, ALU.mult))
                link(V.tensor_reduce(csum[0:S], comb[0:S], axis=AX, op=ALU.add))
                link(V.tensor_scalar(csum[0:S], csum[0:S], 1e-20, None, ALU.add))
                link(V.reciprocal(csum[0:S], csum[0:S]))
                V.scalar_tensor_tensor(comb[0:S], comb[0:S], 2.5, csum[0:S].unsqueeze(2).to_broadcast([S, NB, E]),
                                       ALU.mult, ALU.mult).then_inc(comb_ready, 1)

            with dve.Fori(0, G):
                go()
                for b in range(NB):
                    dve.wait_ge(s_ps, b + 1)
                    link(V.tensor_reduce(nmax[:, 0, b:b + 1], bank[4 + b][0:S, 0:SC], axis=AX, op=ALU.max))
                    V.tensor_scalar(nbias[:, 0, b:b + 1], nmax[:, 0, b:b + 1], -float(D) ** -0.5, None,
                                    ALU.mult).then_inc(max_ready, 1)
                for b in range(NB):
                    dve.wait_ge(t_ps, b + 1)
                    if b >= 2:
                        dve.wait_ge(o_ps, b - 1)
                    V.tensor_copy(pT0[0:CT, b % 2, :], bank[b % 2][0:CT, 0:NT * S]).then_inc(t_copied, 1)
                    if b == 0:
                        dve.wait_ge(x_loaded, 16)
                    if b < 2:
                        norm_stats(xg, range(b * HB, (b + 1) * HB))
                    elif b == 2:
                        norm_means(NB)
                        norm_guess(L0_EPS, NB)
                dve.wait_ge(exp_done, NB)
                link(V.reciprocal(rinv[:, 0, :], rsum[:, 0, :]))
                for _ in range(3):
                    norm_newton(NB)
                norm_apply(xnext, xg)
                dve.wait_ge(x1_free, 1)
                dve.wait_ge(norm_ready, NB)
                for h in range(2):
                    dve.wait_ge(out_ps, h + 1)
                    for b in range(h * HB, (h + 1) * HB):
                        last = V.scalar_tensor_tensor(x1[0:S, b, :], bank[b // 2][0:S, (b % 2) * D:(b % 2 + 1) * D],
                                                      rinv[:, 0, b:b + 1], xb[0:S, b, :], ALU.mult, ALU.add)
                    last.then_inc(inputs_used, 1)
                    dve.wait_ge(inputs_used, h + 1)
                    norm_stats(x1, range(h * HB, (h + 1) * HB))
                norm_means(NB)
                norm_rsqrt(L0_EPS, NB)
                norm_apply(xn, x1)
                for h in range(2):
                    cols = slice(h * TH, (h + 1) * TH)
                    dve.wait_ge(x_hi, h + 1)
                    V.tensor_tensor(xr[:, :, 1, cols], xnT[:, :, cols], xr[:, :, 0, cols], ALU.subtract).then_inc(x_lo, 1)
                dve.wait_ge(sig_ready, 1)
                route_groups()

                def hidden(k):
                    dve.wait_ge(th_ready, k + 1)
                    if k >= 2:
                        dve.wait_ge(h2_done, k - 1)
                    V.scalar_tensor_tensor(h1[:, k % 2, :], th[:, k % 2, :], 1.0, bank[4 + k % 2][:, 0:T],
                                           ALU.add, ALU.mult).then_inc(h1_done, 1)
                    dve.wait_ge(h1_done, k + 1)
                    if k >= 4:
                        dve.wait_ge(inter_ready, k - 3)
                    V.scalar_tensor_tensor((inter if k < 2 else h2)[:, k % 2, :], h1[:, k % 2, :], 0.5,
                                           bank[6 + k % 2][:, 0:T], ALU.mult, ALU.mult).then_inc(h2_done, 1)

                def combine(k):
                    dve.wait_ge(h2_done, k + 1)
                    dve.wait_ge(cb_ps, k - 1)
                    dve.wait_ge(in_lo, k - 1)
                    V.tensor_tensor(inter[:, k % 2, :], h2[:, k % 2, :], bank[2 + k % 2][:, 0:T], ALU.mult).then_inc(inter_ready, 1)

                hidden(0)
                compare_experts()
                hidden(1)
                route_experts()
                hidden(2)
                dve.wait_ge(combT_ps, 1)
                link(V.tensor_copy(combr[:, 0, :], bank[3][0:E, 0:T]))
                V.tensor_tensor(combr[:, 1, :], bank[3][0:E, 0:T], combr[:, 0, :], ALU.subtract).then_inc(combT_ready, 1)
                for k in range(3, E + 2):
                    hidden(k)
                    combine(k - 1)
                combine(E + 1)
                dve.wait_ge(down_ps, E + 2)
                for h in range(2):
                    V.tensor_tensor(x1[0:S, 2 * h:2 * h + 2, :], bank[h][0:S, :].rearrange("p (b d) -> p b d", b=2),
                                    x1[0:S, 2 * h:2 * h + 2, :], ALU.add).then_inc(result, 1)

            def evacuate(name, r, alone=False):
                h = 1 - r % 2
                c = (r - 1) // 2
                bk = projection_bank("values" if name == "values_end" else name, r)
                batches, cols = slice(h * HB, (h + 1) * HB), slice(h * TH, (h + 1) * TH)
                by_batch = bk[0:S, :].rearrange("p (b d) -> p b d", b=HB)
                by_chunk = bk[:, 0:T].rearrange("p (c s) -> p c s", c=DC)
                if name == "values_end" and r <= 0:
                    dve.wait_ge(v_ps, nth(name, r, alone))
                    for par in range(2):
                        halves = "p (s w d) -> p s w d"
                        last = V.tensor_copy(
                            vx[0:S, par, batches, :].rearrange("p b n -> p (b n)").rearrange(halves, w=2, d=XD)[:, :, par, :],
                            bk[0:S, :].rearrange(halves, w=2, d=XD)[:, :, par, :])
                    last.then_inc(v_ready, 1)
                elif name == "keys" and r in SHARED_KEYS:
                    dve.wait_ge(k_ps, nth(name, r, alone))
                    for j, o in [(j, o) for j in (2, 3) for o in range(DC)]:
                        p = slice(32 * j, 32 * j + 32)
                        last = V.tensor_scalar(
                            keys[p, o, batches, j, :], bk[p, o * TH:(o + 1) * TH].rearrange("p (b s) -> p b s", b=HB),
                            ewc[p, c, 1:2], be_kv[p, 0, c, o:o + 1], ALU.mult, ALU.add)
                    last.then_inc(k_shared, 1)
                elif name == "turn":
                    dve.wait_ge(turned, nth(name, r, alone))
                    V.tensor_copy((ynT if r <= 0 else node[0])[:, :, cols], by_chunk).then_inc(xnT_ready, 1)
                elif name == "queries" and r >= 1:
                    dve.wait_ge(q_ps, nth(name, r, alone))
                    V.tensor_scalar(qhT[:, 0, :, cols], by_chunk, float(FD) ** -0.5, None, ALU.mult).then_inc(q_ready, 1)
                elif name == "edge":
                    dve.wait_ge(e_ps, r)
                    for o in range(DC):
                        last = V.tensor_scalar(node[c + 1][:, o, cols], by_chunk[:, o, :], ewc[:, c, 0:1],
                                               be_q[:, c, o:o + 1], ALU.mult, ALU.add)
                    last.then_inc(e_ready, 1)
                elif name == "out":
                    dve.wait_ge(out_ps, nth(name, r, alone))
                    if r <= 2:
                        dve.wait_ge(bias_added, 1)
                        V.tensor_tensor(x3[0:S, batches, :], by_batch, x3[0:S, batches, :], ALU.add).then_inc(x3_ready, 1)
                    else:
                        for o in range(DC):
                            last = V.scalar_tensor_tensor(node[c][:, o, cols], by_chunk[:, o, :], actw[:, c - 1:c],
                                                          node[c][:, o, cols], ALU.mult, ALU.add)
                        last.then_inc(node_ready, 1)

            def take_output(r):
                h, c = 1 - r % 2, (r - 1) // 2
                dve.wait_ge(o_ps, SETS[r - 1][-1][0] + 1)
                for o in range(DC):
                    bias = bv1[:, o:o + 1] if r <= 2 else be_kv[:, 1, c - 1, o:o + 1]
                    last = V.tensor_scalar(aT[:, o, h * TH:(h + 1) * TH], bank[6][:, o * TH:(o + 1) * TH], bias, None,
                                           ALU.add)
                last.then_inc(o_ready, 1)

            def copy_probs(n):
                dve.wait_ge(t_ps, n + 1)
                if n >= SLOTS:
                    dve.wait_ge(o_ps, n - SLOTS + 1)
                V.tensor_copy(pT[0:S, n % SLOTS, :], bank[3][0:S, 0:T]).then_inc(t_copied, 1)

            def invert_sums(n):
                dve.wait_ge(exp_done, n + 1)
                if n >= RING:
                    dve.wait_ge(normed, n - RING + 1)
                V.reciprocal(rinv[:, n % RING, :], rsum[:, n % RING, :]).then_inc(rinv_ready, 1)

            def norm_step(at):
                for r, when in NORM_X3.items():
                    batches = slice((r - 1) * HB, r * HB)
                    if at == when[0]:
                        dve.wait_ge(x3_ready, r)
                        norm_stats(x3[:, batches])
                    if at == when[1]:
                        norm_guess(L0_EPS, HB)
                        norm_newton(HB)
                    for part in when[2:4]:
                        if at == part:
                            norm_newton(HB)
                    if at == when[4]:
                        norm_apply(yn[:, batches], x3[:, batches])

            def norm_slot(slot):
                if slot == 0:
                    dve.wait_ge(fin_ready, 2)
                if slot == NORM_STEPS:
                    dve.wait_ge(loaded, 16 * (1 + DC))
                if 0 <= slot < NORM_STEPS:
                    norm_part(yf, yf, DAG_EPS, slot)
                elif NORM_STEPS <= slot < 2 * NORM_STEPS:
                    norm_part(yn, yg, L0_EPS, slot - NORM_STEPS)

            go()
            dve.wait_ge(loaded, 16 * (1 + DC))
            layernorm(yn, yg, L0_EPS)
            dve.wait_ge(zeroed, 1)
            for name in ("values_end", "turn"):
                evacuate(name, -1, alone=True)
            with dve.Fori(0, G):
                go()
                for w in range(WINDOWS):
                    for i in range(steps(w) + 1):
                        t = i - lag(w)
                        if i == 0 and w:
                            copy_probs(SETS[w - 1][-1][0])
                        due = pieces(w).get(0, []) if i == 2 else []
                        due = due + (pieces(w).get(i - 1, []) if i >= 2 else [])
                        for name, r in due:
                            evacuate(name, r)
                        if i < steps(w):
                            norm_step((w, i))
                        if i == 1 and w >= 3:
                            invert_sums(SETS[w][0][0])
                        if i < len(SETS[w]):
                            n = SETS[w][i][0]
                            dve.wait_ge(s_ps, n + 1)
                            V.tensor_reduce(nbias[:, n % RING, :], bank[n % 3][0:S, 0:T].rearrange(
                                "p (j s) -> p j s", j=STRIPS), axis=AX, op=ALU.max, negate=True).then_inc(max_ready, 1)
                        if i == 1 and w:
                            take_output(w)
                        if (1 if w < 3 else 2) <= i <= len(SETS[w]):
                            invert_sums(SETS[w][i - 1][0])
                        if 0 <= t < len(SETS[w]) - 1:
                            copy_probs(SETS[w][t][0])
                        if (w, i) == (2, 5):
                            V.tensor_copy(rs_t[:, 0:1], rs_y[:, 0:1]).then_inc(inputs_used, 1)
                        if i == 0:
                            norm_slot(2 * (w - NORM_FROM))
                        if i == 5:
                            norm_slot(2 * (w - NORM_FROM) + 1)
                copy_probs(SETS[-1][-1][0])
                take_output(LAST)
            go()
            evacuate("out", LAST, alone=True)
            dve.wait_ge(fin_ready, 2)
            layernorm(yf, yf, DAG_EPS)

        @block.gpsimd
        def _(pool):
            def go():
                pool.wait_ge(go_pool, 1)
                pool.sem_clear(go_pool)

            def rows_add(dst, src, bias, done):
                nc.gpsimd.tensor_tensor(dst[0:S], src[0:S], bias[:].unsqueeze(1).to_broadcast([S, NB, D]),
                                        ALU.add).then_inc(done, 1)

            go()
            rows_add(xb, xg, bias0, bias_added)

            def low_gu(k):
                pool.wait_ge(gu_hi, k + 1)
                for i, w in enumerate((w_gate, w_up)):
                    last = nc.gpsimd.tensor_tensor(w_gu[:, k % 2, i, :, 1, :], w[:, k], w_gu[:, k % 2, i, :, 0, :],
                                                   ALU.subtract)
                last.then_inc(gu_lo, 1)

            def low_inter(k):
                pool.wait_ge(in_hi, k + 1)
                nc.gpsimd.tensor_tensor(inr[:, k % 2, 1, :], inter[:, k % 2, :], inr[:, k % 2, 0, :],
                                        ALU.subtract).then_inc(in_lo, 1)

            with pool.Fori(0, G):
                go()
                low_gu(0)
                low_gu(1)
                pool.wait_ge(x_loaded, 16)
                pool.wait_ge(inputs_used, 2)
                rows_add(xb, xg, bias0, bias_added)
                for k in range(E + 2):
                    if k + 2 < E + 2:
                        low_gu(k + 2)
                    if k >= 1:
                        low_inter(k - 1)
                    pool.wait_ge(dn_hi, k + 1)
                    nc.gpsimd.tensor_tensor(w_dn[:, k % 2, 1, :], w_down[:, k], w_dn[:, k % 2, 0, :],
                                            ALU.subtract).then_inc(dn_lo, 1)
                low_inter(E + 1)

            go()
            nc.gpsimd.memset(keys[:], 0.0)
            nc.gpsimd.memset(vx[0:S], 0.0).then_inc(zeroed, 1)
            nc.gpsimd.tensor_copy(ident_h[0:S], ident[0:S, 0:S])
            nc.gpsimd.tensor_copy(causal_h[0:S].rearrange("p (j s) -> p j s", j=STRIPS),
                                  causal[:].unsqueeze(1).to_broadcast([S, STRIPS, S]))
            for tile in (aT, node[NODES], res):
                last = nc.gpsimd.memset(tile[:], 0.0)
            last.then_inc(zeroed, 1)

            def finish(normalized):
                pool.wait_ge(norm_ready, normalized)
                nc.gpsimd.tensor_tensor(yf[0:S], yf[0:S], ln_g[:].unsqueeze(1).to_broadcast([S, NB, D]),
                                        ALU.mult).then_inc(scaled, 1)
                pool.wait_ge(scaled, 1)
                nc.gpsimd.tensor_tensor(yf[0:S], yf[0:S], res[0:S], ALU.add).then_inc(result, 1)

            with pool.Fori(0, G):
                go()
                rows_add(x3, yg, bo1, bias_added)
                for w in range(WINDOWS):
                    for n, *_ in SETS[w]:
                        pool.wait_ge(rinv_ready, n + 1)
                        if n >= SLOTS:
                            pool.wait_ge(t_ps, n - SLOTS + 1)
                        nc.gpsimd.tensor_tensor(
                            pn[0:S, n % SLOTS, :].rearrange("p (j s) -> p j s", j=STRIPS),
                            pr[0:S, n % SLOTS, :].rearrange("p (j s) -> p j s", j=STRIPS),
                            rinv[:, n % RING, :].unsqueeze(2).to_broadcast([S, STRIPS, S]), ALU.mult).then_inc(normed, 1)
                    if w == FINAL_DONE:
                        finish(NORMS["final"] + NB)
                    if w == 8:
                        pool.wait_ge(x3_ready, 2)
                        pool.wait_ge(result, 1)
                        rows_add(res, x3, ln_b, bias_added)
            go()
            finish(NB)


def kernel(**inputs):
    from concourse import bacc
    from concourse.bass_utils import run_bass_kernel_spmd

    f = {k: np.asarray(v) for k, v in inputs.items()}

    def t(w):
        return np.swapaxes(w, -1, -2)

    def col(b):
        return t(b.reshape(*b.shape[:-1], DC, P))

    x = f["x"].reshape(B * S, D)
    ctx = f["ctx_1024"].reshape(B * SC, D)
    arrays = {"x": x, "ctx": ctx, "ctxT": t(ctx)}
    for name in ("L0_xattn_Wq", "L0_xattn_Wk", "L0_xattn_Wv", "L0_xattn_bo", "L0_ffn_gate_kernel", "L0_ffn_gate_bias",
                 "L0_ffn_w_gate", "L0_ffn_w_up", "L0_ffn_w_down", "L0_ffn_sw_gate", "L0_ffn_sw_up", "L0_ffn_sw_down",
                 "L1_xattn_bo", "L1_ffn_ew", "L1_ffn_act_w", "L1_ffn_We", "L1_ffn_Wq", "L1_ffn_Wk", "L1_ffn_Wv",
                 "L1_ffn_Wo", "L1_ffn_ln_g", "L1_ffn_ln_b"):
        arrays[name] = f[name]
    for name in ("L0_xattn_Wo", "L1_xattn_Wq", "L1_xattn_Wk", "L1_xattn_Wv", "L1_xattn_Wo", "L1_ffn_We"):
        arrays[name + "T"] = t(f[name])
    for name in ("L0_xattn_bq", "L0_xattn_bv", "L1_xattn_bq", "L1_xattn_bk", "L1_xattn_bv"):
        arrays[name] = col(f[name])
    arrays["L1_ffn_beT"] = col(f["L1_ffn_be"])
    i = np.arange(E)
    arrays["c_ident"] = np.eye(P, dtype=np.float32)
    arrays["c_causal"] = np.where(np.arange(S)[None, :] > np.arange(S)[:, None], MASKED, 0.0).astype(np.float32)
    arrays["c_half_mask"] = np.stack([(np.arange(P) // XD % 2 == par) for par in range(2)], 1).astype(np.float32)
    arrays["c_earlier"] = (i[None, :] < i[:, None]).astype(np.float32).reshape(-1)
    arrays["c_later_n"] = (E - 1 - i).astype(np.float32)
    arrays = {k: np.ascontiguousarray(v) for k, v in arrays.items()}

    nc = bacc.Bacc("TRN2", target_bir_lowering=False, num_devices=1)
    aps = {k: nc.dram_tensor(f"in_{k}", v.shape, mybir.dt.from_np(v.dtype), kind="ExternalInput").ap()
           for k, v in arrays.items()}
    out = nc.dram_tensor("out", (B * S, D), F32, kind="ExternalOutput").ap()
    build(nc, aps, out)
    r = run_bass_kernel_spmd(nc, [{f"in_{k}": v for k, v in arrays.items()}], core_ids=[0])
    return r.results[0]["out"].reshape(B, S, D)
```
